# Optimizing a Trainium2 kernel written in Bass

```python
import numpy as np
import jax
import jax.numpy as jnp

def _softmax(x, axis=-1):
    return jax.nn.softmax(x, axis=axis)

def _gelu(x):
    return jax.nn.gelu(x, approximate=True)

def _silu(x):
    return jax.nn.silu(x)

def _sigmoid(x):
    return jax.nn.sigmoid(x)

def _layernorm(x, axis=-1, eps=1e-05):
    m = jnp.mean(x, axis=axis, keepdims=True)
    v = jnp.var(x, axis=axis, keepdims=True)
    return (x - m) / jnp.sqrt(v + eps)

def _scatter_add(tgt, idx, src, axis=0):
    return tgt.at[idx].add(src)

def _segment_sum(src, seg, n):
    return jax.ops.segment_sum(src, seg, n)
kernel_name = 'mk_macaron_d1_jaxref_r4_5462de'

def setup_inputs(seed: int=0):
    np.random.seed(seed)
    _w = jnp.asarray

    def _L0_attn_setup():
        import jax, jax.numpy as jnp
        import numpy as np
        from jax import lax
        B, L, D = (4, 512, 512)
        R = 512
        DH = D // 4
        key = jax.random.key(seed)
        ks = jax.random.split(key, 12)
        s = 0.02
        x = jax.random.normal(ks[0], (B, L, D), dtype=jnp.float32)
        Wu = jax.random.normal(ks[1], (R, D), dtype=jnp.float32) * s
        bu = jnp.zeros((R,), dtype=jnp.float32)
        Wv = jax.random.normal(ks[2], (R, D), dtype=jnp.float32) * s
        bv = jnp.zeros((R,), dtype=jnp.float32)
        Wg1 = jax.random.normal(ks[3], (DH, D), dtype=jnp.float32) * s
        bg1 = jnp.zeros((DH,), dtype=jnp.float32)
        Wg2 = jax.random.normal(ks[4], (R, DH), dtype=jnp.float32) * s
        bg2 = jnp.zeros((R,), dtype=jnp.float32)
        conv_w = jax.random.normal(ks[5], (D, 1, 3), dtype=jnp.float32) * s
        conv_b = jnp.zeros((D,), dtype=jnp.float32)
        return {'x': x, 'Wu': Wu, 'bu': bu, 'Wv': Wv, 'bv': bv, 'Wg1': Wg1, 'bg1': bg1, 'Wg2': Wg2, 'bg2': bg2, 'conv_w': conv_w, 'conv_b': conv_b}
    _L0_attn_in = _L0_attn_setup()

    def _L0_ffn_setup():
        import math
        import jax, jax.numpy as jnp
        import numpy as np
        NUM_EXPERTS = 8
        HIDDEN = 512
        INTER = 2048
        CAP_FACTOR = 1.25
        MIN_CAP = 4
        B, S = (4, 512)

        def _capacity(num_tokens: int, num_experts: int) -> int:
            cap = math.floor(CAP_FACTOR * num_tokens / num_experts)
            cap += cap % 2
            return max(cap, MIN_CAP)
        key = jax.random.key(seed)
        k1, k2, k3, k4 = jax.random.split(key, 4)
        std_h = math.sqrt(0.1 / HIDDEN)
        std_i = math.sqrt(0.1 / INTER)
        inputs = jax.random.normal(k1, (B, S, HIDDEN), dtype=jnp.float32)
        gate_weight = jax.random.normal(k2, (NUM_EXPERTS, HIDDEN), dtype=jnp.float32) * std_h
        wi = jax.random.normal(k3, (NUM_EXPERTS, HIDDEN, INTER), dtype=jnp.float32) * std_h
        wo = jax.random.normal(k4, (NUM_EXPERTS, INTER, HIDDEN), dtype=jnp.float32) * std_i
        return {'inputs': inputs, 'gate_weight': gate_weight, 'wi': wi, 'wo': wo}
    _L0_ffn_in = _L0_ffn_setup()
    _d = {'L0_attn_x': _L0_attn_in['x'], 'L0_attn_Wu': _L0_attn_in['Wu'], 'L0_attn_bu': _L0_attn_in['bu'], 'L0_attn_Wv': _L0_attn_in['Wv'], 'L0_attn_bv': _L0_attn_in['bv'], 'L0_attn_Wg1': _L0_attn_in['Wg1'], 'L0_attn_bg1': _L0_attn_in['bg1'], 'L0_attn_Wg2': _L0_attn_in['Wg2'], 'L0_attn_bg2': _L0_attn_in['bg2'], 'L0_attn_conv_w': _L0_attn_in['conv_w'], 'L0_attn_conv_b': _L0_attn_in['conv_b'], 'L0_ffn_gate_weight': _L0_ffn_in['gate_weight'], 'L0_ffn_wi': _L0_ffn_in['wi'], 'L0_ffn_wo': _L0_ffn_in['wo']}
    _x0 = _d['L0_attn_x']
    _d['L0_attn_x'] = jax.random.normal(jax.random.fold_in(jax.random.key(seed), 1), (2, 1024, 512), dtype=_x0.dtype)
    del _x0
    return _d

def reference(L0_attn_x, L0_attn_Wu, L0_attn_bu, L0_attn_Wv, L0_attn_bv, L0_attn_Wg1, L0_attn_bg1, L0_attn_Wg2, L0_attn_bg2, L0_attn_conv_w, L0_attn_conv_b, L0_ffn_gate_weight, L0_ffn_wi, L0_ffn_wo):

    def _L0_attn_ref(x, Wu, bu, Wv, bv, Wg1, bg1, Wg2, bg2, conv_w, conv_b):
        import jax, jax.numpy as jnp
        import numpy as np
        from jax import lax
        B, L, D = (4, 512, 512)
        R = 512
        DH = D // 4
        xc = jnp.transpose(x, (0, 2, 1))
        t = lax.conv_general_dilated(xc, conv_w, window_strides=(1,), padding=[(1, 1)], dimension_numbers=('NCH', 'OIH', 'NCH'), feature_group_count=D)
        t_out = jnp.transpose(t + conv_b[None, :, None], (0, 2, 1))
        u = jnp.einsum('bld,rd->blr', x, Wu) + bu
        v = jnp.einsum('bld,rd->blr', x, Wv) + bv
        h = jax.nn.relu(jnp.einsum('bld,hd->blh', x, Wg1) + bg1)
        gates = jax.nn.sigmoid(jnp.einsum('blh,rh->blr', h, Wg2) + bg2)
        u_gated = u * gates
        v_gated = v * gates
        k_cumsum = jnp.cumsum(u_gated, axis=1)
        global_out = k_cumsum * v_gated
        uv_term = jnp.einsum('blr,rd->bld', global_out, Wu.T[:R, :])
        return t_out + uv_term

    def _L0_ffn_ref(inputs, gate_weight, wi, wo):
        import math
        import jax, jax.numpy as jnp
        import numpy as np
        NUM_EXPERTS = 8
        HIDDEN = 512
        INTER = 2048
        CAP_FACTOR = 1.25
        MIN_CAP = 4
        B, S = (4, 512)

        def _capacity(num_tokens: int, num_experts: int) -> int:
            cap = math.floor(CAP_FACTOR * num_tokens / num_experts)
            cap += cap % 2
            return max(cap, MIN_CAP)
        b, s, h = inputs.shape
        tokens = inputs.reshape(-1, h)
        T = tokens.shape[0]
        E = gate_weight.shape[0]
        C = _capacity(T, E)
        logits = tokens.astype(jnp.float32) @ gate_weight.astype(jnp.float32).T
        probs = jax.nn.softmax(logits, axis=-1)
        top1 = jnp.argmax(logits, axis=-1)
        mask = jax.nn.one_hot(top1, E, dtype=jnp.int32)
        ranks = jnp.cumsum(mask, axis=0) - 1
        mask = mask * (ranks < C).astype(jnp.int32)
        ranks_tok = jnp.sum(mask * ranks, axis=-1)
        ranks_oh = jax.nn.one_hot(ranks_tok, C, dtype=jnp.float32)
        weight = mask.astype(probs.dtype) * probs
        combine_weights = weight[:, :, None] * ranks_oh[:, None, :]
        sec_mask = jax.lax.stop_gradient(combine_weights != 0).astype(inputs.dtype)
        dispatch = jnp.einsum('tec,th->ech', sec_mask, tokens)
        hmid = jnp.einsum('ech,ehi->eci', dispatch, wi)
        hmid = jax.nn.gelu(hmid, approximate=False)
        eout = jnp.einsum('eci,eih->ech', hmid, wo)
        out = jnp.einsum('tec,ech->th', combine_weights.astype(inputs.dtype), eout)
        return out.reshape(b, s, h)
    x = L0_attn_x
    x = x + 0.5 * _L0_ffn_ref(_layernorm(x, axis=-1), L0_ffn_gate_weight, L0_ffn_wi, L0_ffn_wo)
    x = x + _L0_attn_ref(_layernorm(x, axis=-1), L0_attn_Wu, L0_attn_bu, L0_attn_Wv, L0_attn_bv, L0_attn_Wg1, L0_attn_bg1, L0_attn_Wg2, L0_attn_bg2, L0_attn_conv_w, L0_attn_conv_b)
    x = x + 0.5 * _L0_ffn_ref(_layernorm(x, axis=-1), L0_ffn_gate_weight, L0_ffn_wi, L0_ffn_wo)
    return x

_drawn_inputs = setup_inputs


def setup_inputs(seed=0):
    import zlib

    import numpy as np

    out = dict(_drawn_inputs(seed))
    spreads = {'L0_attn_bu': (0.0, 0.1),
     'L0_attn_bv': (0.0, 0.1),
     'L0_attn_bg1': (0.0, 0.729),
     'L0_attn_bg2': (0.0, 0.1),
     'L0_attn_conv_b': (0.0, 0.1)}
    factors = {'L0_attn_conv_w': 5.368, 'L0_ffn_gate_weight': 8.0, 'L0_ffn_wi': 8.0, 'L0_ffn_wo': 8.0}
    for name, (base, spread) in spreads.items():
        noise = np.random.default_rng([zlib.crc32(name.encode()), seed]).standard_normal(out[name].shape)
        drawn = base * np.exp(spread * noise) if base else spread * noise
        out[name] = jnp.asarray(drawn.astype(out[name].dtype))
    for name, factor in factors.items():
        out[name] = (out[name] * factor).astype(out[name].dtype)
    return out
```

```python
from contextlib import ExitStack

import concourse.bass as bass
from concourse import mybir

ALU = mybir.AluOpType
ACT = mybir.ActivationFunctionType
F32 = mybir.dt.float32
F32R = mybir.dt.float32r
BF16 = mybir.dt.bfloat16
I32 = mybir.dt.int32
AX_X = mybir.AxisListType.X

P = 128
BATCH, SEQ, D = 2, 1024, 512
T = BATCH * SEQ
TILES = T // P
DC = D // P
E, INTER = 8, 2048
CAP = 320
SLOTS = E * CAP
PARTS = [(0, 128), (128, 128), (256, 64)]
GROUP = 4
GROUPS = TILES // GROUP
GT = GROUP * P
UNIT = 512
UNITS = INTER // UNIT
HALF = 256
STEPS = INTER // HALF
ICS = HALF // P
DH = D // 4
EPS = 1e-5
KB = 1024

GATE0, BU0, BV0, BG20, CB0, BG10, CW0, SMALL = 0, 32, 36, 40, 44, 48, 49, 64


def build_kernel(nc, x, wuT, wvT, wg1T, wg2T, small_in, wi, wo, out):
    x_tiles = x.rearrange("b (n p) d -> p (b n) d", p=P)
    out_tiles = out.rearrange("b (n p) d -> p (b n) d", p=P)
    disp = nc.dram_tensor("disp", [SLOTS + T, D], F32, kind="Internal").ap()
    eout = nc.dram_tensor("eout", [SLOTS, D], F32, kind="Internal").ap()

    with ExitStack() as ctx:
        base = (nc.sbuf_base + 31) // 32 * 32
        top = [base]

        def at(name, shape, dt, offset):
            return nc.alloc_sbuf_tensor_at(name, shape, dt, offset=offset)

        def size(shape, dt):
            n = 2 if dt is BF16 else 4
            for s in shape[1:]:
                n *= s
            return (n + 31) // 32 * 32

        def put(name, shape, dt):
            t = at(name, shape, dt, top[0])
            top[0] += size(shape, dt)
            return t

        xt = put("xt", [P, TILES, D], F32)
        xn = put("xn", [P, TILES, D], F32)
        wu = [put(f"wu{k}", [P, DC, D], F32R) for k in "hl"]
        wv = [put(f"wv{k}", [P, DC, D], F32R) for k in "hl"]
        raw_wi = [put(f"raw_wi{k}", [P, DC, UNIT], F32) for k in range(2)]
        ident = put("ident", [P, P], F32)
        tri = put("tri", [P, P], BF16)
        ones = put("ones", [P, P], BF16)
        desc = put("desc", [P, E, TILES], F32)
        slot0 = put("slot0", [P, E, TILES], F32)
        carry_on = put("carry_on", [P, E * TILES], F32)
        spare = put("spare", [P, TILES], F32)
        small = put("small", [P, SMALL], F32)
        expo = put("expo", [P, TILES], F32)
        mv = put("mv", [P, TILES, 2], F32)
        var = put("var", [P, TILES], F32)
        rstd = put("rstd", [P, TILES], F32)
        weight = put("weight", [P, TILES], F32)
        to_row = put("to_row", [P, TILES], I32)
        from_row = put("from_row", [P, TILES], I32)
        carry = put("carry", [P, DC], F32)
        stats = put("stats", [P, GROUP, 6], F32)
        one_col = put("one_col", [P, 1], F32)

        shared = top[0]
        raw_wo = [put(f"raw_wo{k}", [P, DC, UNIT], F32) for k in range(2)]
        wih = put("wih", [P, 2, DC, HALF], F32R)
        wil = put("wil", [P, 2, DC, HALF], F32R)
        woh = put("woh", [P, 2, ICS, D], F32R)
        wol = put("wol", [P, 2, ICS, D], F32R)
        gel = put("gel", [P, 2, ICS, CAP], F32)
        hth = put("hth", [P, 2, ICS, CAP], F32R)
        htl = put("htl", [P, 2, ICS, CAP], F32R)
        a_dt = top[0]
        dth = put("dth", [P, DC, CAP], F32R)
        dtl = put("dtl", [P, DC, CAP], F32R)
        dtok = put("dtok", [P, len(PARTS), D], F32)
        a_eo = top[0]
        eoT = put("eoT", [P, DC, CAP], F32)
        eotok = put("eotok", [P, len(PARTS), D], F32)
        ffn_top = top[0]
        zeros = at("zeros", [P, SLOTS // P // 4 * D], F32, a_dt)
        xTt = at("xTt", [P, 2, DC, P], F32, a_eo)
        top[0] = a_eo + 4 * KB
        lg = put("lg", [P, E, TILES], F32)
        sel = put("sel", [P, E, TILES], F32)
        oh = put("oh", [P, E, TILES], F32)
        ohb = put("ohb", [P, E, TILES], BF16)
        cnt = put("cnt", [P, E, TILES], F32)
        incl = put("incl", [P, E * TILES], F32)
        r8 = put("r8", [P, E, TILES], F32)
        t16 = put("t16", [P, 8, TILES], F32)
        top[0] = shared
        xT = put("xT", [P, DC, BATCH, SEQ + 2], F32)
        xTh = put("xTh", [P, DC, GT], F32R)
        xTl = put("xTl", [P, DC, GT], F32R)
        glh = put("glh", [P, DC, GT], F32R)
        gll = put("gll", [P, DC, GT], F32R)
        wg1 = [put(f"wg1{k}", [P, DC, DH], F32R) for k in "hl"]
        wg2 = [put(f"wg2{k}", [P, D], F32R) for k in "hl"]
        hh = put("hh", [P, GT], F32R)
        hl = put("hl", [P, GT], F32R)
        gate = put("gate", [P, GT], F32)
        ug = put("ug", [P, GT], F32)
        vg = [put(f"vg{k}", [P, GT], F32) for k in range(2)]
        a_cv = top[0]
        convT = put("convT", [P, DC, GT], F32)
        raw_g1 = at("raw_g1", [P, DC, DH], F32, a_cv)
        raw_g2 = at("raw_g2", [P, D], F32, a_cv + 2 * KB)
        assert max(top[0], ffn_top) <= nc.sbuf_usable_end, (top[0], ffn_top, nc.sbuf_usable_end)

        acc = [ctx.enter_context(nc.psum_tensor(f"acc{k}", [P, 512], F32)) for k in range(4)]
        psH = [ctx.enter_context(nc.psum_tensor(f"psH{k}", [P, 512], F32)) for k in range(2)]
        psT = [ctx.enter_context(nc.psum_tensor(f"psT{k}", [P, 512], F32)) for k in range(2)]
        ps_logit = acc[0][:, 0:TILES * E]
        ps_count = acc[1][:, 0:TILES * E]
        ps_total = acc[2][:, 0:TILES * E]

        def sem(name):
            return ctx.enter_context(nc.semaphore(name))

        class Layer:

            def __init__(self, n):
                self.var_done = sem(f"var_done{n}")
                self.rstd_done = sem(f"rstd_done{n}")
                self.xn_done = sem(f"xn_done{n}")
                self.xT_done = sem(f"xT_done{n}")
                self.xT_copied = sem(f"xT_copied{n}")
                self.logits_done = sem(f"logits_done{n}")
                self.diff_done = sem(f"diff_done{n}")
                self.exp_done = sem(f"exp_done{n}")
                self.oh_done = sem(f"oh_done{n}")
                self.rank_done = sem(f"rank_done{n}")
                self.rows_done = sem(f"rows_done{n}")
                self.scattered = sem(f"scattered{n}")
                self.wi_in = [sem(f"wi_in{n}_{k}") for k in range(2)]
                self.wo_in = [sem(f"wo_in{n}_{k}") for k in range(2)]
                self.wi_hi = sem(f"wi_hi{n}")
                self.wi_lo = sem(f"wi_lo{n}")
                self.wo_hi = sem(f"wo_hi{n}")
                self.wo_lo = sem(f"wo_lo{n}")
                self.h_ready = sem(f"h_ready{n}")
                self.gelu_done = sem(f"gelu_done{n}")
                self.ht_hi = sem(f"ht_hi{n}")
                self.ht_lo = sem(f"ht_lo{n}")
                self.mm2_done = sem(f"mm2_done{n}")
                self.acc_done = sem(f"acc_done{n}")
                self.eoT_act = sem(f"eoT_act{n}")
                self.eoT_dve = sem(f"eoT_dve{n}")
                self.dtok_in = sem(f"dtok_in{n}")
                self.tokT_done = sem(f"tokT_done{n}")
                self.dt_hi = sem(f"dt_hi{n}")
                self.dt_lo = sem(f"dt_lo{n}")
                self.outT_done = sem(f"outT_done{n}")
                self.out_act = sem(f"out_act{n}")
                self.out_dve = sem(f"out_dve{n}")
                self.eout_out = sem(f"eout_out{n}")
                self.eotok_free = sem(f"eotok_free{n}")
                self.y_in = [sem(f"y_in{n}_{k}") for k in range(GROUPS)]

        layers = [Layer(0), Layer(1)]
        x_in = [sem(f"x_in{k}") for k in range(GROUPS)]
        small_loaded = sem("small_loaded")
        uv_raw_in = [sem("wu_raw_in"), sem("wv_raw_in")]
        uv_hi = sem("uv_hi")
        uv_lo = sem("uv_lo")
        g_raw_in = sem("g_raw_in")
        g_hi = sem("g_hi")
        g_lo = sem("g_lo")
        pool_const = sem("pool_const")
        dve_const = sem("dve_const")
        zero_out = sem("zero_out")
        dve_seq = sem("dve_seq")
        n_var = sem("n_var")
        n_rstd = sem("n_rstd")
        n_xn = sem("n_xn")
        n_T = sem("n_T")
        n_xT = sem("n_xT")
        n_pad = sem("n_pad")
        n_xTh = sem("n_xTh")
        n_xTl = sem("n_xTl")
        p_ring = sem("p_ring")
        a_h = sem("a_h")
        d_hh = sem("d_hh")
        d_hl = sem("d_hl")
        a_gate = sem("a_gate")
        d_ug = sem("d_ug")
        d_vg = sem("d_vg")
        d_glob = sem("d_glob")
        a_glh = sem("a_glh")
        d_gll = sem("d_gll")
        a_conv = sem("a_conv")
        d_conv = sem("d_conv")
        p_conv = sem("p_conv")
        d_addc = sem("d_addc")
        p_uv = sem("p_uv")
        d_addu = sem("d_addu")
        out_ready = sem("out_ready")
        out_done = sem("out_done")

        block = ctx.enter_context(nc.Block())

        RING = 1 + 3 * DC

        @block.sync
        def _(sp):
            sp.dma_start(small[:, :], small_in).then_inc(small_loaded, 16)
            for g in range(GROUPS):
                sp.dma_start(xt[:, g * GROUP:(g + 1) * GROUP, :],
                             x_tiles[:, g * GROUP:(g + 1) * GROUP, :]).then_inc(x_in[g], 16)
            sp.dma_start(raw_wi[0][:, :, :], wuT.rearrange("(c p) r -> p c r", p=P)).then_inc(uv_raw_in[0], 16)
            sp.dma_start(raw_wi[1][:, :, :], wvT.rearrange("(c p) r -> p c r", p=P)).then_inc(uv_raw_in[1], 16)
            sp.wait_ge(dve_const, 1)
            for k in range(4):
                rows = SLOTS // 4
                sp.dma_start(disp[k * rows:(k + 1) * rows, :].rearrange("(p r) d -> p (r d)", p=P),
                             zeros[:, :]).then_inc(zero_out, 16)

            def load_wi(s, e, u, k):
                sp.dma_start(raw_wi[k][:, :, :],
                             wi[bass.ds(e, 1), :, u * UNIT:(u + 1) * UNIT]
                             .rearrange("a (c p) i -> p (a c) i", p=P)).then_inc(s.wi_in[k], 16)

            def load_wo(s, e, u, k):
                sp.dma_start(raw_wo[k][:, :, :],
                             wo[bass.ds(e, 1), u * UNIT:(u + 1) * UNIT, :]
                             .rearrange("a (c p) d -> p (a c) d", p=P)).then_inc(s.wo_in[k], 16)

            for n, s in enumerate(layers):
                if n == 0:
                    sp.wait_ge(uv_lo, 2)
                else:
                    sp.wait_ge(layers[0].wi_lo, E * STEPS)
                for k in range(2):
                    load_wi(s, 0, k, k)
                if n == 1:
                    sp.wait_ge(d_addu, TILES)
                for k in range(2):
                    load_wo(s, 0, k, k)

                def ahead(e, k, s=s):
                    done = e * STEPS + 2 * (k + 1)
                    sp.wait_ge(s.wi_lo, done)
                    load_wi(s, e + (k + 2) // UNITS, (k + 2) % UNITS, k % 2)
                    sp.wait_ge(s.wo_lo, done)
                    load_wo(s, e + (k + 2) // UNITS, (k + 2) % UNITS, k % 2)

                with sp.Fori(0, E - 1) as e:
                    for k in range(UNITS):
                        ahead(e, k)
                for k in range(UNITS - 2):
                    ahead(E - 1, k)
                if n == 0:
                    sp.wait_ge(s.eotok_free, 1 + E)
                    sp.dma_start(raw_g1[:, :, :], wg1T.rearrange("(c p) r -> p c r", p=P)).then_inc(g_raw_in, 16)
                    sp.dma_start(raw_g2[:, :], wg2T).then_inc(g_raw_in, 16)
            for g in range(GROUPS):
                sp.wait_ge(out_ready, g + 1)
                sp.dma_start(out_tiles[:, g * GROUP:(g + 1) * GROUP, :],
                             xt[:, g * GROUP:(g + 1) * GROUP, :]).then_inc(out_done, 16)
            sp.wait_ge(out_done, 16 * GROUPS)

        @block.gpsimd
        def _(pool):
            pool.memset(ident[:, :], 0.0).then_inc(pool_const, 1)
            pool.memset(tri[:, :], 1.0).then_inc(pool_const, 1)
            pool.memset(ones[:, :], 1.0).then_inc(pool_const, 1)
            pool.memset(expo[:, :], -0.5).then_inc(pool_const, 1)
            pool.wait_ge(pool_const, 4)
            pool.affine_select(out=ident[:, :], in_=ident[:, :], compare_op=ALU.not_equal, fill=1.0,
                               base=0, pattern=[[-1, P]], channel_multiplier=1).then_inc(pool_const, 1)
            pool.affine_select(out=tri[:, :], in_=tri[:, :], compare_op=ALU.is_ge, fill=0.0,
                               base=0, pattern=[[1, P]], channel_multiplier=-1).then_inc(pool_const, 1)
            pool.iota(desc[:, :, :], [[-1, E], [0, TILES]], base=E, channel_multiplier=0,
                      allow_small_or_imprecise_dtypes=True).then_inc(pool_const, 1)
            pool.iota(slot0[:, :, :], [[CAP, E], [0, TILES]], base=-1, channel_multiplier=0,
                      allow_small_or_imprecise_dtypes=True).then_inc(pool_const, 1)
            pool.iota(spare[:, :], [[P, TILES]], base=SLOTS, channel_multiplier=1,
                      allow_small_or_imprecise_dtypes=True).then_inc(pool_const, 1)

            def power(g, var_sem, rstd_sem):
                pool.wait_ge(var_sem, g + 1)
                q = slice(g * GROUP, (g + 1) * GROUP)
                pool.tensor_tensor(rstd[:, q], var[:, q], expo[:, q], ALU.pow).then_inc(rstd_sem, 1)

            def load_tokens(s, e):
                pool.dma_start(dtok[:, 0:2, :], disp[bass.ds(e * CAP, 256), :]
                               .rearrange("(c p) d -> p c d", p=P)).then_inc(s.dtok_in, 16)
                pool.dma_start(dtok[0:64, 2, :], disp[bass.ds(e * CAP + 256, 64), :]).then_inc(s.dtok_in, 16)

            for n, s in enumerate(layers):
                pool.sem_inc(s.eotok_free, 1)
                if n == 0:
                    for g in range(GROUPS):
                        power(g, s.var_done, s.rstd_done)
                else:
                    power(0, n_var, n_rstd)
                    for g in range(GROUPS):
                        if g + 1 < GROUPS:
                            power(g + 1, n_var, n_rstd)
                        power(g, s.var_done, s.rstd_done)
                pool.wait_ge(s.rows_done, 1)
                if n == 0:
                    pool.wait_ge(zero_out, 64)
                for t in range(TILES):
                    pool.indirect_dma_start(disp[:, :], bass.IndirectOffsetOnAxis(ap=to_row[:, t:t + 1], axis=0),
                                            xn[:, t, :], None).then_inc(s.scattered, 16)
                pool.wait_ge(s.scattered, 16 * TILES)
                load_tokens(s, 0)

                def expert(e, last, s=s):
                    if not last:
                        pool.wait_ge(s.tokT_done, DC * e + DC)
                        load_tokens(s, e + 1)
                    pool.wait_ge(s.out_act, 1 + 2 * e + 2)
                    pool.wait_ge(s.out_dve, e + 1)
                    pool.dma_start(eout[bass.ds(e * CAP, 256), :].rearrange("(c p) d -> p c d", p=P),
                                   eotok[:, 0:2, :]).then_inc(s.eout_out, 16)
                    pool.dma_start(eout[bass.ds(e * CAP + 256, 64), :], eotok[0:64, 2, :]).then_inc(s.eout_out, 16)
                    pool.wait_ge(s.eout_out, 32 * e + 32)
                    pool.sem_inc(s.eotok_free, 1)

                with pool.Fori(0, E - 1) as e:
                    expert(e, False)
                expert(E - 1, True)
                if n == 0:
                    for b in range(BATCH):
                        for c in (0, SEQ + 1):
                            pool.memset(xT[:, :, b, c:c + 1], 0.0).then_inc(n_pad, 1)
                for t in range(TILES):
                    pool.indirect_dma_start(xn[:, t, :], None, eout[:, :],
                                            bass.IndirectOffsetOnAxis(ap=from_row[:, t:t + 1], axis=0)
                                            ).then_inc(s.y_in[t // GROUP], 16)

        @block.scalar
        def _(act):
            copy = ACT.Copy
            for n, s in enumerate(layers):
                if n == 0:
                    for k, w in enumerate((wu, wv)):
                        act.wait_ge(uv_raw_in[k], 16)
                        act.activation(w[0][:, :, :], raw_wi[k][:, :, :], copy).then_inc(uv_hi, 1)
                act.sem_inc(s.gelu_done, ICS)
                act.sem_inc(s.eoT_act, 1)
                act.sem_inc(s.out_act, 1)
                for t in range(TILES):
                    act.wait_ge(s.xT_done, t + 1)
                    if t >= 2:
                        act.wait_ge(s.logits_done, t - 1)
                    act.activation(xTt[:, t % 2, :, :], psT[t % 2][:, :].rearrange("p (c q) -> p c q", c=DC),
                                   copy).then_inc(s.xT_copied, 1)
                act.wait_ge(s.diff_done, 1)
                act.activation(sel[:, :, :], sel[:, :, :], ACT.Exp).then_inc(s.exp_done, 1)

                def wi_split(e, step, s=s):
                    k = (step // 2) % 2
                    if step % 2 == 0:
                        act.wait_ge(s.wi_in[k], 32 * e + 16 * (step // 4 + 1))
                    act.wait_ge(s.h_ready, ICS * STEPS * e + ICS * (step + 1))
                    act.activation(wih[:, step % 2, :, :],
                                   raw_wi[k][:, :, (step % 2) * HALF:(step % 2 + 1) * HALF],
                                   copy).then_inc(s.wi_hi, 1)

                def wo_split(e, step, s=s):
                    k = (step // 2) % 2
                    if step % 2 == 0:
                        act.wait_ge(s.wo_in[k], 32 * e + 16 * (step // 4 + 1))
                    act.wait_ge(s.mm2_done, STEPS * e + step + 1)
                    act.activation(woh[:, step % 2, :, :],
                                   raw_wo[k][:, (step % 2) * ICS:(step % 2 + 1) * ICS, :],
                                   copy).then_inc(s.wo_hi, 1)

                wi_split(0, 0)
                wi_split(0, 1)
                wo_split(0, 0)

                def expert(e, last, s=s):
                    for step in range(STEPS):
                        act.wait_ge(s.ht_lo, STEPS * e + step + 1)
                        for j in range(ICS):
                            ic = ICS * step + j
                            act.wait_ge(s.h_ready, 2 * ICS + ICS * STEPS * e + ic + 1)
                            act.activation(gel[:, step % 2, j, :], psH[j][:, 0:CAP],
                                           ACT.Gelu).then_inc(s.gelu_done, 1)
                        if not last or step + 2 < STEPS:
                            wi_split(e, step + 2)
                        if not last or step + 1 < STEPS:
                            wo_split(e, step + 1)
                    for c in (0, 2):
                        act.wait_ge(s.acc_done, DC * e + c + 1)
                        act.activation(eoT[:, c, :], acc[c][:, 0:CAP], copy).then_inc(s.eoT_act, 1)
                    act.wait_ge(s.eotok_free, e + 1)
                    act.wait_ge(s.outT_done, 3 * e + 1)
                    act.activation(eotok[:, 0, :], psT[0][:, :], copy).then_inc(s.out_act, 1)
                    act.wait_ge(s.outT_done, 3 * e + 3)
                    act.activation(eotok[0:64, 2, :], psH[1][0:64, :], copy).then_inc(s.out_act, 1)

                with act.Fori(0, E - 1) as e:
                    expert(e, False)
                expert(E - 1, True)

                if n == 1:
                    break
                act.wait_ge(g_raw_in, 32)
                act.activation(wg1[0][:, :, :], raw_g1[:, :, :], copy).then_inc(g_hi, 1)
                act.activation(wg2[0][:, :], raw_g2[:, :], copy).then_inc(g_hi, 1)

                def copy_xT(g):
                    b, q = g // 2, 1 + (g % 2) * GT
                    for c in range(DC):
                        act.wait_ge(n_T, DC * g + c + 1)
                        act.activation(xT[:, c, b, q:q + GT], psT[c % 2][:, :], copy).then_inc(n_xT, 1)

                def split_xT(g):
                    b, q = g // 2, 1 + (g % 2) * GT
                    act.wait_ge(n_xT, DC * (g + 1))
                    if g >= 1:
                        act.wait_ge(p_ring, RING * g)
                    for c in range(DC):
                        act.activation(xTh[:, c, :], xT[:, c, b, q:q + GT], copy).then_inc(n_xTh, 1)

                def conv_mid(g):
                    b, q = g // 2, 1 + (g % 2) * GT
                    if g == 0:
                        act.wait_ge(g_lo, 2)
                    else:
                        act.wait_ge(p_conv, GROUP * g)
                    for c in range(DC):
                        act.activation(convT[:, c, :], xT[:, c, b, q:q + GT], ACT.Identity,
                                       bias=small[:, CB0 + c:CB0 + c + 1],
                                       scale=small[:, CW0 + 3 * c + 1:CW0 + 3 * c + 2]).then_inc(a_conv, 1)

                copy_xT(0)
                split_xT(0)
                for g in range(GROUPS):
                    act.wait_ge(p_ring, RING * g + 1)
                    if g >= 1:
                        act.wait_ge(d_glob, DC * g)
                    act.activation(ug[:, :], acc[(RING * g) % 4][:, :], ACT.Relu,
                                   bias=small[:, BG10:BG10 + 1]).then_inc(a_h, 1)
                    for c in range(DC):
                        i = DC * g + c
                        u = RING * g + 1 + 3 * c
                        if c == 3 and g + 1 < GROUPS:
                            copy_xT(g + 1)
                        act.wait_ge(p_ring, u + 1)
                        if i >= 1:
                            act.wait_ge(d_vg, i)
                        act.activation(gate[:, :], acc[u % 4][:, :], ACT.Sigmoid,
                                       bias=small[:, BG20 + c:BG20 + c + 1]).then_inc(a_gate, 1)
                        if c == 3:
                            conv_mid(g)
                        if c >= 1:
                            act.wait_ge(d_glob, i)
                            if g >= 1:
                                act.wait_ge(p_uv, GROUP * g)
                            act.activation(glh[:, c - 1, :], vg[(c - 1) % 2][:, :], copy).then_inc(a_glh, 1)
                    act.wait_ge(d_glob, DC * (g + 1))
                    act.activation(glh[:, DC - 1, :], vg[(DC - 1) % 2][:, :], copy).then_inc(a_glh, 1)
                    if g + 1 < GROUPS:
                        split_xT(g + 1)

        @block.vector
        def _(dve):
            seq = [0]

            def then(ins):
                ins.then_inc(dve_seq, 1)
                seq[0] += 1

            def settle():
                dve.wait_ge(dve_seq, seq[0])

            def lo(out, full, hi):
                return dve.tensor_tensor(out, full, hi.bitcast(F32), ALU.subtract)

            def norm(g, var_sem, rstd_sem, xn_sem):
                q = slice(g * GROUP, (g + 1) * GROUP)
                for j in range(GROUP):
                    then(dve.bn_stats(stats[:, j, :], xt[:, g * GROUP + j, :]))
                settle()
                for j in range(GROUP):
                    then(dve.bn_aggr(mv[:, g * GROUP + j, :], stats[:, j, :]))
                settle()
                dve.tensor_scalar(var[:, q], mv[:, q, 1], EPS, None, ALU.add).then_inc(var_sem, 1)
                dve.wait_ge(rstd_sem, g + 1)
                for j in range(GROUP):
                    t = g * GROUP + j
                    ins = dve.tensor_scalar(xn[:, t, :], xt[:, t, :], mv[:, t, 0:1], rstd[:, t:t + 1],
                                            ALU.subtract, ALU.mult)
                ins.then_inc(xn_sem, 1)

            def add_ffn(g, s):
                dve.wait_ge(s.y_in[g], 16 * GROUP)
                for j in range(GROUP):
                    t = g * GROUP + j
                    ins = dve.scalar_tensor_tensor(xt[:, t, :], xn[:, t, :], weight[:, t:t + 1], xt[:, t, :],
                                                   ALU.mult, ALU.add)
                    if s is layers[0]:
                        then(ins)
                return ins

            def rows(s):
                by_t = "p e t -> p t e"
                each = [P, E, TILES]

                def over(k):
                    return t16[:, k:k + 1, :].to_broadcast(each)

                dve.wait_ge(s.logits_done, TILES)
                then(dve.tensor_copy(lg[:, :, :], ps_logit.rearrange("p (t e) -> p e t", e=E)))
                settle()
                then(dve.tensor_reduce(t16[:, 0, :], lg[:, :, :].rearrange(by_t), AX_X, ALU.max))
                settle()
                dve.tensor_tensor(sel[:, :, :], lg[:, :, :], over(0), ALU.subtract).then_inc(s.diff_done, 1)
                then(dve.tensor_tensor(oh[:, :, :], lg[:, :, :], over(0), ALU.is_equal))
                settle()
                then(dve.tensor_tensor(r8[:, :, :], oh[:, :, :], desc[:, :, :], ALU.mult))
                settle()
                then(dve.tensor_reduce(t16[:, 1, :], r8[:, :, :].rearrange(by_t), AX_X, ALU.max))
                settle()
                then(dve.tensor_tensor(oh[:, :, :], desc[:, :, :], over(1), ALU.is_equal))
                settle()
                dve.tensor_copy(ohb[:, :, :], oh[:, :, :]).then_inc(s.oh_done, 1)
                dve.wait_ge(s.exp_done, 1)
                then(dve.tensor_reduce(t16[:, 2, :], sel[:, :, :].rearrange(by_t), AX_X, ALU.add))
                settle()
                then(dve.reciprocal(t16[:, 3, :], t16[:, 2, :]))
                dve.wait_ge(s.rank_done, 1)
                then(dve.tensor_tensor_scan(incl[:, :], carry_on[:, :], ps_total, 0.0, ALU.mult, ALU.add))
                settle()
                flat = cnt[:, :, :].rearrange("p e t -> p (e t)")
                then(dve.tensor_tensor(incl[:, :], incl[:, :], ps_total, ALU.subtract))
                settle()
                then(dve.tensor_tensor(flat, incl[:, :], ps_count, ALU.add))
                settle()
                then(dve.tensor_tensor(r8[:, :, :], cnt[:, :, :], oh[:, :, :], ALU.mult))
                settle()
                then(dve.tensor_reduce(t16[:, 4, :], r8[:, :, :].rearrange(by_t), AX_X, ALU.add))
                then(dve.tensor_tensor(cnt[:, :, :], cnt[:, :, :], slot0[:, :, :], ALU.add))
                settle()
                then(dve.tensor_tensor(r8[:, :, :], cnt[:, :, :], oh[:, :, :], ALU.mult))
                then(dve.tensor_scalar(t16[:, 6, :], t16[:, 4, :], float(CAP), None, ALU.is_le))
                settle()
                then(dve.tensor_reduce(t16[:, 5, :], r8[:, :, :].rearrange(by_t), AX_X, ALU.add))
                then(dve.scalar_tensor_tensor(weight[:, :], t16[:, 3, :], 0.5, t16[:, 6, :], ALU.mult, ALU.mult))
                settle()
                then(dve.tensor_tensor(t16[:, 7, :], t16[:, 5, :], t16[:, 6, :], ALU.mult))
                then(dve.tensor_tensor(t16[:, 5, :], t16[:, 5, :], spare[:, :], ALU.subtract))
                settle()
                then(dve.tensor_copy(from_row[:, :], t16[:, 7, :]))
                then(dve.tensor_tensor(t16[:, 5, :], t16[:, 5, :], t16[:, 6, :], ALU.mult))
                settle()
                then(dve.tensor_tensor(t16[:, 5, :], t16[:, 5, :], spare[:, :], ALU.add))
                settle()
                dve.tensor_copy(to_row[:, :], t16[:, 5, :]).then_inc(s.rows_done, 1)

            dve.memset(zeros[:, :], 0.0).then_inc(dve_const, 1)
            then(dve.memset(one_col[:, :], 1.0))
            then(dve.memset(carry_on[:, :], 1.0))
            settle()
            then(dve.memset(carry_on[:, :].rearrange("p (e t) -> p e t", e=E)[:, :, 0:1], 0.0))

            for n, s in enumerate(layers):
                dve.sem_inc(s.ht_lo, 2)
                dve.sem_inc(s.eoT_dve, 1)
                if n == 0:
                    for g in range(GROUPS):
                        dve.wait_ge(x_in[g], 16)
                        norm(g, s.var_done, s.rstd_done, s.xn_done)
                    for k, w in enumerate((wu, wv)):
                        dve.wait_ge(uv_hi, k + 1)
                        lo(w[1][:, :, :], raw_wi[k][:, :, :], w[0][:, :, :]).then_inc(uv_lo, 1)
                    dve.wait_ge(pool_const, 9)
                rows(s)

                def wi_split(e, step, s=s):
                    k = (step // 2) % 2
                    dve.wait_ge(s.wi_hi, STEPS * e + step + 1)
                    lo(wil[:, step % 2, :, :], raw_wi[k][:, :, (step % 2) * HALF:(step % 2 + 1) * HALF],
                       wih[:, step % 2, :, :]).then_inc(s.wi_lo, 1)

                def wo_split(e, step, s=s):
                    k = (step // 2) % 2
                    dve.wait_ge(s.wo_hi, STEPS * e + step + 1)
                    lo(wol[:, step % 2, :, :], raw_wo[k][:, (step % 2) * ICS:(step % 2 + 1) * ICS, :],
                       woh[:, step % 2, :, :]).then_inc(s.wo_lo, 1)

                def tokens(e, c, s=s):
                    ps = psT[c % 2][:, 0:CAP]
                    dve.wait_ge(s.tokT_done, DC * e + c + 1)
                    dve.tensor_copy(dth[:, c, :], ps).then_inc(s.dt_hi, 1)
                    dve.wait_ge(s.dt_hi, DC * e + c + 1)
                    lo(dtl[:, c, :], ps, dth[:, c, :]).then_inc(s.dt_lo, 1)

                wi_split(0, 0)
                wi_split(0, 1)
                wo_split(0, 0)
                for c in range(DC):
                    tokens(0, c)

                def expert(e, last, s=s):
                    for step in range(STEPS):
                        k = step % 2
                        dve.wait_ge(s.gelu_done, ICS + ICS * (STEPS * e + step + 1))
                        dve.wait_ge(s.mm2_done, STEPS * e + step + 1)
                        dve.tensor_copy(hth[:, k, :, :], gel[:, k, :, :]).then_inc(s.ht_hi, 1)
                        dve.wait_ge(s.ht_hi, STEPS * e + step + 1)
                        lo(htl[:, k, :, :], gel[:, k, :, :], hth[:, k, :, :]).then_inc(s.ht_lo, 1)
                        if step == STEPS - 1 and not last:
                            tokens(e + 1, 0)
                            tokens(e + 1, 1)
                        if not last or step + 2 < STEPS:
                            wi_split(e, step + 2)
                        if not last or step + 1 < STEPS:
                            wo_split(e, step + 1)
                    if not last:
                        tokens(e + 1, 2)
                        tokens(e + 1, 3)
                    for c in (1, 3):
                        dve.wait_ge(s.acc_done, DC * e + c + 1)
                        dve.tensor_copy(eoT[:, c, :], acc[c][:, 0:CAP]).then_inc(s.eoT_dve, 1)
                    dve.wait_ge(s.eotok_free, e + 1)
                    dve.wait_ge(s.outT_done, 3 * e + 2)
                    dve.tensor_copy(eotok[:, 1, :], psT[1][:, :]).then_inc(s.out_dve, 1)

                with dve.Fori(0, E - 1) as e:
                    expert(e, False)
                expert(E - 1, True)

                if n == 1:
                    for g in range(GROUPS):
                        add_ffn(g, s).then_inc(out_ready, 1)
                    break
                nxt = layers[1]

                def new_group(g):
                    add_ffn(g, s)
                    settle()
                    norm(g, n_var, n_rstd, n_xn)

                def xT_lo(g):
                    b, q = g // 2, 1 + (g % 2) * GT
                    for c in range(DC):
                        dve.wait_ge(n_xTh, DC * g + c + 1)
                        lo(xTl[:, c, :], xT[:, c, b, q:q + GT], xTh[:, c, :]).then_inc(n_xTl, 1)

                def glob_lo(i):
                    c = i % DC
                    dve.wait_ge(a_glh, i + 1)
                    lo(gll[:, c, :], vg[c % 2][:, :], glh[:, c, :]).then_inc(d_gll, 1)

                def taps(g):
                    b, q = g // 2, 1 + (g % 2) * GT
                    dve.wait_ge(n_pad, 4)
                    dve.wait_ge(n_xT, DC * min(g + 2 - g % 2, GROUPS))
                    for k, shift in ((0, -1), (2, 1)):
                        for c in range(DC):
                            dve.wait_ge(a_conv, DC * g + c + 1)
                            ins = dve.scalar_tensor_tensor(
                                convT[:, c, :], xT[:, c, b, q + shift:q + shift + GT],
                                small[:, CW0 + 3 * c + k:CW0 + 3 * c + k + 1], convT[:, c, :],
                                ALU.mult, ALU.add)
                            if k == 0:
                                then(ins)
                            else:
                                ins.then_inc(d_conv, 1)
                        settle()

                dve.wait_ge(g_hi, 2)
                lo(wg1[1][:, :, :], raw_g1[:, :, :], wg1[0][:, :, :]).then_inc(g_lo, 1)
                lo(wg2[1][:, :], raw_g2[:, :], wg2[0][:, :]).then_inc(g_lo, 1)
                new_group(0)
                xT_lo(0)
                for g in range(GROUPS):
                    dve.wait_ge(a_h, g + 1)
                    dve.tensor_copy(hh[:, :], ug[:, :]).then_inc(d_hh, 1)
                    dve.wait_ge(d_hh, g + 1)
                    lo(hl[:, :], ug[:, :], hh[:, :]).then_inc(d_hl, 1)
                    for c in range(DC):
                        i = DC * g + c
                        u = RING * g + 1 + 3 * c
                        dve.wait_ge(a_gate, i + 1)
                        dve.wait_ge(p_ring, u + 2)
                        if c == 0:
                            dve.wait_ge(d_hl, g + 1)
                        else:
                            dve.wait_ge(d_glob, i)
                        dve.scalar_tensor_tensor(ug[:, :], acc[(u + 1) % 4][:, :], small[:, BU0 + c:BU0 + c + 1],
                                                 gate[:, :], ALU.add, ALU.mult).then_inc(d_ug, 1)
                        if c >= 1:
                            glob_lo(i - 1)
                        dve.wait_ge(d_ug, i + 1)
                        start = 0.0 if g % 2 == 0 else carry[:, c:c + 1]
                        then(dve.tensor_tensor_scan(ug[:, :], one_col[:, :].to_broadcast([P, GT]), ug[:, :],
                                                    start, ALU.mult, ALU.add))
                        dve.wait_ge(p_ring, u + 3)
                        dve.scalar_tensor_tensor(vg[c % 2][:, :], acc[(u + 2) % 4][:, :],
                                                 small[:, BV0 + c:BV0 + c + 1],
                                                 gate[:, :], ALU.add, ALU.mult).then_inc(d_vg, 1)
                        settle()
                        dve.wait_ge(d_vg, i + 1)
                        if g % 2 == 0:
                            then(dve.tensor_copy(carry[:, c:c + 1], ug[:, GT - 1:GT]))
                        dve.tensor_tensor(vg[c % 2][:, :], vg[c % 2][:, :], ug[:, :], ALU.mult).then_inc(d_glob, 1)
                        if c == 0 and g + 1 < GROUPS:
                            new_group(g + 1)
                    glob_lo(DC * g + DC - 1)
                    taps(g)
                    for j in range(GROUP):
                        w = GROUP * g + j
                        dve.wait_ge(p_conv, w + 1)
                        dve.tensor_tensor(xt[:, w, :], psT[j % 2][:, :], xt[:, w, :], ALU.add).then_inc(d_addc, 1)
                    if g + 1 < GROUPS:
                        xT_lo(g + 1)
                    for j in range(GROUP):
                        w = GROUP * g + j
                        dve.wait_ge(p_uv, w + 1)
                        dve.wait_ge(d_addc, w + 1)
                        dve.tensor_tensor(xt[:, w, :], psH[j % 2][:, :], xt[:, w, :], ALU.add).then_inc(d_addu, 1)
                    dve.wait_ge(d_addu, GROUP * (g + 1))
                    norm(g, nxt.var_done, nxt.rstd_done, nxt.xn_done)

        @block.tensor
        def _(pe):
            def product(out, lhs, rhs, first, last):
                (lh, ll), (rh, rl) = lhs, rhs
                pe.matmul(out, lh, rh, start=first, stop=False)
                pe.matmul(out, lh, rl, start=False, stop=False)
                return pe.matmul(out, ll, rh, start=False, stop=last)

            pe.wait_ge(pool_const, 9)
            for n, s in enumerate(layers):
                pe.sem_inc(s.h_ready, 2 * ICS)
                pe.sem_inc(s.mm2_done, 2)

                def turn(t, s=s):
                    pe.wait_ge(s.xn_done, t // GROUP + 1)
                    if t >= 2:
                        pe.wait_ge(s.xT_copied, t - 1)
                    for c in range(DC):
                        ins = pe.transpose(psT[t % 2][:, c * P:(c + 1) * P], xn[:, t, c * P:(c + 1) * P], ident[:, :])
                    ins.then_inc(s.xT_done, 1)

                def logits(t, s=s):
                    pe.wait_ge(s.xT_copied, t + 1)
                    if t == 0:
                        pe.wait_ge(small_loaded, 16)
                    for c in range(DC):
                        ins = pe.matmul(ps_logit[:, t * E:(t + 1) * E], xTt[:, t % 2, c, :],
                                        small[:, GATE0 + c * E:GATE0 + (c + 1) * E],
                                        start=(c == 0), stop=(c == DC - 1))
                    ins.then_inc(s.logits_done, 1)

                turn(0)
                for t in range(1, TILES):
                    turn(t)
                    logits(t - 1)
                logits(TILES - 1)
                pe.wait_ge(s.oh_done, 1)
                pick = ohb[:, :, :].rearrange("p e t -> p (e t)")
                pe.matmul(ps_count, tri[:, :], pick, start=True, stop=True)
                pe.matmul(ps_total, ones[:, :], pick, start=True, stop=True).then_inc(s.rank_done, 1)

                def turn_tokens(e, c, s=s):
                    pe.wait_ge(s.dtok_in, 32 * e + 32)
                    if c >= 2:
                        pe.wait_ge(s.dt_lo, DC * e + c - 1)
                    for k, (q, m) in enumerate(PARTS):
                        ins = pe.transpose(psT[c % 2][:, q:q + m], dtok[0:m, k, c * P:(c + 1) * P], ident[0:m, 0:m])
                    ins.then_inc(s.tokT_done, 1)

                def mm1(e, step, s=s):
                    k = step % 2
                    pe.wait_ge(s.wi_lo, STEPS * e + step + 1)
                    if step == 0:
                        pe.wait_ge(s.dt_lo, DC * e + DC)
                    for j in range(ICS):
                        ic = ICS * step + j
                        pe.wait_ge(s.gelu_done, ICS * STEPS * e + ic + 1)
                        if ic == 1:
                            pe.wait_ge(s.out_act, 1 + 2 * e)
                        for c in range(DC):
                            w = slice(j * P, (j + 1) * P)
                            ins = product(psH[j][:, 0:CAP], (wih[:, k, c, w], wil[:, k, c, w]),
                                          (dth[:, c, :], dtl[:, c, :]), c == 0, c == DC - 1)
                        ins.then_inc(s.h_ready, 1)

                def mm2(e, step, s=s):
                    k = step % 2
                    pe.wait_ge(s.wo_lo, STEPS * e + step + 1)
                    pe.wait_ge(s.ht_lo, 2 + STEPS * e + step + 1)
                    if step == 0:
                        pe.wait_ge(s.eoT_act, 1 + 2 * e)
                        pe.wait_ge(s.eoT_dve, 1 + 2 * e)
                    for c in range(DC):
                        for j in range(ICS):
                            w = slice(c * P, (c + 1) * P)
                            ins = product(acc[c][:, 0:CAP], (woh[:, k, j, w], wol[:, k, j, w]),
                                          (hth[:, k, j, :], htl[:, k, j, :]),
                                          step == 0 and j == 0, step == STEPS - 1 and j == ICS - 1)
                        if step == STEPS - 1 and c < DC - 1:
                            ins.then_inc(s.acc_done, 1)
                    return ins

                def turn_out(e, last, s=s):
                    banks = (psT[0], psT[1], psH[1])
                    if not last:
                        pe.wait_ge(s.dt_lo, DC * (e + 1) + DC)
                    for c in range(DC):
                        if c % 2 == 0:
                            pe.wait_ge(s.eoT_act, 1 + 2 * e + c // 2 + 1)
                        else:
                            pe.wait_ge(s.eoT_dve, 1 + 2 * e + c // 2 + 1)
                        for k, (q, m) in enumerate(PARTS):
                            ins = pe.transpose(banks[k][0:m, c * P:(c + 1) * P], eoT[:, c, q:q + m], ident[:, :])
                            if c == 0 and k == 0:
                                ins.then_inc(s.mm2_done, 1)
                            if c == DC - 1:
                                ins.then_inc(s.outT_done, 1)

                for c in range(DC):
                    turn_tokens(0, c)

                def expert(e, last, s=s):
                    mm1(e, 0)
                    for step in range(1, STEPS):
                        mm1(e, step)
                        if step == STEPS - 1 and not last:
                            turn_tokens(e + 1, 0)
                            turn_tokens(e + 1, 1)
                        mm2(e, step - 1).then_inc(s.mm2_done, 1)
                    if not last:
                        turn_tokens(e + 1, 2)
                        turn_tokens(e + 1, 3)
                    mm2(e, STEPS - 1).then_inc(s.acc_done, 1)
                    turn_out(e, last)

                with pe.Fori(0, E - 1) as e:
                    expert(e, False)
                expert(E - 1, True)

                if n == 1:
                    break
                used = [0]

                def bank():
                    u = used[0]
                    if u >= 4:
                        g, k = divmod(u - 4, RING)
                        if k == 0:
                            pe.wait_ge(a_h, g + 1)
                        else:
                            c, kind = divmod(k - 1, 3)
                            pe.wait_ge((a_gate, d_ug, d_vg)[kind], DC * g + c + 1)
                    used[0] += 1
                    return acc[u % 4][:, :]

                def turn_group(g):
                    pe.wait_ge(n_xn, g + 1)
                    for c in range(DC):
                        if c >= 2:
                            pe.wait_ge(n_xT, DC * g + c - 1)
                        elif g >= 2:
                            pe.wait_ge(d_addc, GROUP * (g - 1))
                        elif g == 1:
                            pe.wait_ge(n_xT, DC)
                        for j in range(GROUP):
                            ins = pe.transpose(psT[c % 2][:, j * P:(j + 1) * P],
                                               xn[:, GROUP * g + j, c * P:(c + 1) * P], ident[:, :])
                        ins.then_inc(n_T, 1)

                turn_group(0)
                for g in range(GROUPS):
                    if g == 0:
                        pe.wait_ge(g_lo, 2)
                        pe.wait_ge(uv_lo, 2)
                    pe.wait_ge(n_xTl, DC * (g + 1))
                    to = bank()
                    for c in range(DC):
                        ins = product(to, (wg1[0][:, c, :], wg1[1][:, c, :]), (xTh[:, c, :], xTl[:, c, :]),
                                      c == 0, c == DC - 1)
                    ins.then_inc(p_ring, 1)

                    def projection(w, c):
                        to = bank()
                        r = slice(c * P, (c + 1) * P)
                        for k in range(DC):
                            ins = product(to, (w[0][:, k, r], w[1][:, k, r]), (xTh[:, k, :], xTl[:, k, :]),
                                          k == 0, k == DC - 1)
                        ins.then_inc(p_ring, 1)

                    for c in range(DC):
                        if c == 0:
                            pe.wait_ge(d_hl, g + 1)
                        to = bank()
                        r = slice(c * P, (c + 1) * P)
                        product(to, (wg2[0][:, r], wg2[1][:, r]), (hh[:, :], hl[:, :]), True, True).then_inc(p_ring, 1)
                        projection(wu, c)
                        projection(wv, c)
                        if c == 2 and g + 1 < GROUPS:
                            turn_group(g + 1)
                    for j in range(GROUP):
                        w = GROUP * g + j
                        if j == 0:
                            pe.wait_ge(d_conv, DC * (g + 1))
                        if j < 2:
                            pe.wait_ge(n_xT, DC * min(g + 2, GROUPS))
                        if w >= 2:
                            pe.wait_ge(d_addc, w - 1)
                        for c in range(DC):
                            ins = pe.transpose(psT[j % 2][:, c * P:(c + 1) * P], convT[:, c, j * P:(j + 1) * P],
                                               ident[:, :])
                        ins.then_inc(p_conv, 1)
                    pe.wait_ge(d_gll, DC * (g + 1))
                    for j in range(GROUP):
                        w = GROUP * g + j
                        if w >= 2:
                            pe.wait_ge(d_addu, w - 1)
                        q = slice(j * P, (j + 1) * P)
                        for c in range(DC):
                            ins = product(psH[j % 2][:, :], (glh[:, c, q], gll[:, c, q]), (wu[0][:, c, :], wu[1][:, c, :]),
                                          c == 0, c == DC - 1)
                        ins.then_inc(p_uv, 1)


def kernel(L0_attn_x, L0_attn_Wu, L0_attn_bu, L0_attn_Wv, L0_attn_bv, L0_attn_Wg1, L0_attn_bg1, L0_attn_Wg2,
           L0_attn_bg2, L0_attn_conv_w, L0_attn_conv_b, L0_ffn_gate_weight, L0_ffn_wi, L0_ffn_wo):
    import numpy as np
    import concourse.bacc as bacc
    from concourse.bass_utils import run_bass_kernel_spmd

    def cols(v):
        v = np.asarray(v).reshape(np.shape(v)[0] // P, P, -1)
        return v.transpose(1, 0, 2).reshape(P, -1)

    small = np.zeros((P, SMALL), np.float32)
    small[:, GATE0:BU0] = cols(np.asarray(L0_ffn_gate_weight).T)
    small[:, BU0:BV0] = cols(L0_attn_bu)
    small[:, BV0:BG20] = cols(L0_attn_bv)
    small[:, BG20:CB0] = cols(L0_attn_bg2)
    small[:, CB0:BG10] = cols(L0_attn_conv_b)
    small[:, BG10:CW0] = cols(L0_attn_bg1)
    small[:, CW0:CW0 + 3 * DC] = cols(np.asarray(L0_attn_conv_w)[:, 0, :])

    arrays = {
        "x": L0_attn_x,
        "wuT": np.asarray(L0_attn_Wu).T,
        "wvT": np.asarray(L0_attn_Wv).T,
        "wg1T": np.asarray(L0_attn_Wg1).T,
        "wg2T": np.asarray(L0_attn_Wg2).T,
        "small": small,
        "wi": L0_ffn_wi,
        "wo": L0_ffn_wo,
    }
    nc = bacc.Bacc("TRN2", target_bir_lowering=False, num_devices=1)
    sent, args = {}, []
    for name, a in arrays.items():
        a = np.ascontiguousarray(a)
        sent[f"in_{name}"] = a
        args.append(nc.dram_tensor(f"in_{name}", a.shape, mybir.dt.from_np(a.dtype), kind="ExternalInput").ap())
    out = nc.dram_tensor("out_x", (BATCH, SEQ, D), F32, kind="ExternalOutput").ap()
    build_kernel(nc, *args, out)
    return run_bass_kernel_spmd(nc, [sent], core_ids=[0]).results[0]["out_x"]
```

```python
from contextlib import ExitStack

import concourse.bass as bass
from concourse import mybir

ALU = mybir.AluOpType
ACT = mybir.ActivationFunctionType
F32 = mybir.dt.float32
F32R = mybir.dt.float32r
BF16 = mybir.dt.bfloat16
I32 = mybir.dt.int32
AX_X = mybir.AxisListType.X

P = 128
BATCH, SEQ, D = 2, 1024, 512
T = BATCH * SEQ
TILES = T // P
DC = D // P
E, INTER = 8, 2048
CAP = 320
SLOTS = E * CAP
PARTS = [(0, 128), (128, 128), (256, 64)]
WIDTHS = (224, 256, 288, CAP)
GROUP = 4
GROUPS = TILES // GROUP
GT = GROUP * P
UNIT = 512
UNITS = INTER // UNIT
HALF = 256
STEPS = INTER // HALF
ICS = HALF // P
DH = D // 4
EPS = 1e-5
KB = 1024

GATE0, BU0, BV0, BG20, CB0, BG10, CW0, SMALL = 0, 32, 36, 40, 44, 48, 49, 64


def build_kernel(nc, x, wuT, wvT, wg1T, wg2T, small_in, wi, wo, out):
    x_tiles = x.rearrange("b (n p) d -> p (b n) d", p=P)
    out_tiles = out.rearrange("b (n p) d -> p (b n) d", p=P)
    disp = nc.dram_tensor("disp", [SLOTS + T, D], F32, kind="Internal").ap()
    eout = nc.dram_tensor("eout", [SLOTS, D], F32, kind="Internal").ap()

    with ExitStack() as ctx:
        base = (nc.sbuf_base + 31) // 32 * 32
        top = [base]

        def at(name, shape, dt, offset):
            return nc.alloc_sbuf_tensor_at(name, shape, dt, offset=offset)

        def size(shape, dt):
            n = 2 if dt is BF16 else 4
            for s in shape[1:]:
                n *= s
            return (n + 31) // 32 * 32

        def put(name, shape, dt):
            t = at(name, shape, dt, top[0])
            top[0] += size(shape, dt)
            return t

        xt = put("xt", [P, TILES, D], F32)
        xn = put("xn", [P, TILES, D], F32)
        wu = [put(f"wu{k}", [P, DC, D], F32R) for k in "hl"]
        wv = [put(f"wv{k}", [P, DC, D], F32R) for k in "hl"]
        ident = put("ident", [P, P], F32)
        tri = put("tri", [P, P], BF16)
        ones = put("ones", [P, P], BF16)
        desc = put("desc", [P, E, GROUP], F32)
        slot0 = put("slot0", [P, E, GROUP], F32)
        spare = put("spare", [P, TILES], F32)
        small = put("small", [P, SMALL], F32)
        expo = put("expo", [P, TILES], F32)
        mv = put("mv", [P, TILES, 2], F32)
        var = put("var", [P, TILES], F32)
        rstd = put("rstd", [P, TILES], F32)
        neg_mean = put("neg_mean", [P, TILES], F32)
        shift = put("shift", [P, TILES], F32)
        weight = put("weight", [P, TILES], F32)
        to_row = put("to_row", [P, TILES], I32)
        from_row = put("from_row", [P, TILES], I32)
        taken = put("taken", [P, E], I32)
        carry = put("carry", [P, DC], F32)
        stats = put("stats", [P, GROUP, 6], F32)
        one_col = put("one_col", [P, 1], F32)

        shared = top[0]
        raw_wi = [put(f"raw_wi{k}", [P, DC, UNIT], F32) for k in range(2)]
        raw_wo = [put(f"raw_wo{k}", [P, DC, UNIT], F32) for k in range(2)]
        wih = put("wih", [P, 2, DC, HALF], F32R)
        wil = put("wil", [P, 2, DC, HALF], F32R)
        woh = put("woh", [P, 2, ICS, D], F32R)
        wol = put("wol", [P, 2, ICS, D], F32R)
        gel = put("gel", [P, 2, ICS, CAP], F32)
        hth = put("hth", [P, 2, ICS, CAP], F32R)
        htl = put("htl", [P, 2, ICS, CAP], F32R)
        a_dt = top[0]
        dth = put("dth", [P, DC, CAP], F32R)
        dtl = put("dtl", [P, DC, CAP], F32R)
        dtok = put("dtok", [P, len(PARTS), D], F32)
        a_eo = top[0]
        eoT = put("eoT", [P, DC, CAP], F32)
        eotok = put("eotok", [P, len(PARTS), D], F32)
        ffn_top = top[0]
        zeros = at("zeros", [P, SLOTS // P // 4 * D], F32, a_dt)
        xTt = at("xTt", [P, 2, DC, P], F32, a_eo)
        top[0] = a_eo + 4 * KB
        each = [P, E, GROUP]
        lg = put("lg", each, F32)
        sel = put("sel", [P, 2, E, GROUP], F32)
        ohb = put("ohb", [P, 2, E, GROUP], BF16)
        r8 = put("r8", each, F32)
        t4 = put("t4", [P, 9, GROUP], F32)
        before = put("before", [P, 2, E], BF16)
        so_far = put("so_far", [P, E], F32)
        top[0] = shared
        xT = put("xT", [P, DC, SEQ + 2], F32)
        xTh = put("xTh", [P, 2, DC, GT], F32R)
        xTl = put("xTl", [P, 2, DC, GT], F32R)
        glh = put("glh", [P, 2, DC, GT], F32R)
        gll = put("gll", [P, 2, DC, GT], F32R)
        wg1 = [put(f"wg1{k}", [P, DC, DH], F32R) for k in "hl"]
        wg2 = [put(f"wg2{k}", [P, D], F32R) for k in "hl"]
        hh = put("hh", [P, GT], F32R)
        hl = put("hl", [P, GT], F32R)
        gate = put("gate", [P, GT], F32)
        ug = put("ug", [P, GT], F32)
        vg = [put(f"vg{k}", [P, GT], F32) for k in range(2)]
        a_cv = top[0]
        convT = put("convT", [P, DC, GT], F32)
        raw_g1 = at("raw_g1", [P, DC, DH], F32, a_cv)
        raw_g2 = at("raw_g2", [P, D], F32, a_cv + 2 * KB)
        assert max(top[0], ffn_top) <= nc.sbuf_usable_end, (top[0], ffn_top, nc.sbuf_usable_end)

        acc = [ctx.enter_context(nc.psum_tensor(f"acc{k}", [P, 512], F32)) for k in range(4)]
        psH = [ctx.enter_context(nc.psum_tensor(f"psH{k}", [P, 512], F32)) for k in range(2)]
        psT = [ctx.enter_context(nc.psum_tensor(f"psT{k}", [P, 512], F32)) for k in range(2)]
        ps_logit = [acc[k][:, 0:GROUP * E] for k in (0, 1)]
        ps_rank = [acc[k][:, 0:GROUP * E] for k in (2, 3)]

        def sem(name):
            return ctx.enter_context(nc.semaphore(name))

        class Layer:

            def __init__(self, n):
                self.var_done = sem(f"var_done{n}")
                self.rstd_done = sem(f"rstd_done{n}")
                self.xn_done = sem(f"xn_done{n}")
                self.xT_done = sem(f"xT_done{n}")
                self.xT_copied = sem(f"xT_copied{n}")
                self.logits_done = sem(f"logits_done{n}")
                self.lg_copied = sem(f"lg_copied{n}")
                self.diff_done = sem(f"diff_done{n}")
                self.exp_done = sem(f"exp_done{n}")
                self.oh_done = sem(f"oh_done{n}")
                self.before_done = sem(f"before_done{n}")
                self.rank_done = sem(f"rank_done{n}")
                self.rank_used = sem(f"rank_used{n}")
                self.taken_done = sem(f"taken_done{n}")
                self.rows_done = sem(f"rows_done{n}")
                self.scattered = sem(f"scattered{n}")
                self.wi_in = [sem(f"wi_in{n}_{k}") for k in range(2)]
                self.wo_in = [sem(f"wo_in{n}_{k}") for k in range(2)]
                self.wi_hi = sem(f"wi_hi{n}")
                self.wi_lo = sem(f"wi_lo{n}")
                self.wo_hi = sem(f"wo_hi{n}")
                self.wo_lo = sem(f"wo_lo{n}")
                self.h_ready = sem(f"h_ready{n}")
                self.gelu_done = sem(f"gelu_done{n}")
                self.ht_hi = sem(f"ht_hi{n}")
                self.ht_lo = sem(f"ht_lo{n}")
                self.mm2_done = sem(f"mm2_done{n}")
                self.acc_done = sem(f"acc_done{n}")
                self.eoT_done = sem(f"eoT_done{n}")
                self.dtok_in = sem(f"dtok_in{n}")
                self.tokT_done = sem(f"tokT_done{n}")
                self.dt_hi = sem(f"dt_hi{n}")
                self.dt_lo = sem(f"dt_lo{n}")
                self.outT_done = sem(f"outT_done{n}")
                self.out_act = sem(f"out_act{n}")
                self.out_dve = sem(f"out_dve{n}")
                self.eout_out = sem(f"eout_out{n}")
                self.eotok_free = sem(f"eotok_free{n}")
                self.y_in = [sem(f"y_in{n}_{k}") for k in range(GROUPS)]

        layers = [Layer(0), Layer(1)]
        x_in = [sem(f"x_in{k}") for k in range(GROUPS)]
        small_loaded = sem("small_loaded")
        uv_raw_in = [sem("wu_raw_in"), sem("wv_raw_in")]
        uv_hi = sem("uv_hi")
        uv_lo = sem("uv_lo")
        g_raw_in = sem("g_raw_in")
        g_hi = sem("g_hi")
        g_lo = sem("g_lo")
        pool_const = sem("pool_const")
        dve_const = sem("dve_const")
        zero_out = sem("zero_out")
        dve_seq = sem("dve_seq")
        n_var = sem("n_var")
        n_rstd = sem("n_rstd")
        n_xn = sem("n_xn")
        n_T = sem("n_T")
        n_xT = sem("n_xT")
        n_pad = sem("n_pad")
        n_xTh = sem("n_xTh")
        n_xTl = sem("n_xTl")
        p_ring = sem("p_ring")
        a_h = sem("a_h")
        d_hh = sem("d_hh")
        d_hl = sem("d_hl")
        a_gate = sem("a_gate")
        d_ug = sem("d_ug")
        d_vg = sem("d_vg")
        d_glob = sem("d_glob")
        a_glh = sem("a_glh")
        d_gll = sem("d_gll")
        a_conv = sem("a_conv")
        d_tap = sem("d_tap")
        d_conv = sem("d_conv")
        p_conv = sem("p_conv")
        d_addc = sem("d_addc")
        p_uv = sem("p_uv")
        d_addu = sem("d_addu")
        out_ready = sem("out_ready")
        out_done = sem("out_done")

        block = ctx.enter_context(nc.Block())

        RING = 1 + 3 * DC

        @block.sync
        def _(sp):
            sp.dma_start(small[:, :], small_in).then_inc(small_loaded, 16)
            for g in range(GROUPS):
                sp.dma_start(xt[:, g * GROUP:(g + 1) * GROUP, :],
                             x_tiles[:, g * GROUP:(g + 1) * GROUP, :]).then_inc(x_in[g], 16)
            sp.dma_start(raw_wi[0][:, :, :], wuT.rearrange("(c p) r -> p c r", p=P)).then_inc(uv_raw_in[0], 16)
            sp.dma_start(raw_wi[1][:, :, :], wvT.rearrange("(c p) r -> p c r", p=P)).then_inc(uv_raw_in[1], 16)
            sp.wait_ge(dve_const, 1)
            for k in range(4):
                rows = SLOTS // 4
                sp.dma_start(disp[k * rows:(k + 1) * rows, :].rearrange("(p r) d -> p (r d)", p=P),
                             zeros[:, :]).then_inc(zero_out, 16)

            def load_wi(s, e, u, k):
                sp.dma_start(raw_wi[k][:, :, :],
                             wi[bass.ds(e, 1), :, u * UNIT:(u + 1) * UNIT]
                             .rearrange("a (c p) i -> p (a c) i", p=P)).then_inc(s.wi_in[k], 16)

            def load_wo(s, e, u, k):
                sp.dma_start(raw_wo[k][:, :, :],
                             wo[bass.ds(e, 1), u * UNIT:(u + 1) * UNIT, :]
                             .rearrange("a (c p) d -> p (a c) d", p=P)).then_inc(s.wo_in[k], 16)

            for n, s in enumerate(layers):
                if n == 0:
                    sp.wait_ge(uv_lo, 2)
                else:
                    sp.wait_ge(d_addu, TILES)
                for k in range(2):
                    load_wi(s, 0, k, k)
                for k in range(2):
                    load_wo(s, 0, k, k)

                def ahead(e, k, s=s):
                    done = e * STEPS + 2 * (k + 1)
                    sp.wait_ge(s.wi_lo, done)
                    load_wi(s, e + (k + 2) // UNITS, (k + 2) % UNITS, k % 2)
                    sp.wait_ge(s.wo_lo, done)
                    load_wo(s, e + (k + 2) // UNITS, (k + 2) % UNITS, k % 2)

                with sp.Fori(0, E - 1) as e:
                    for k in range(UNITS):
                        ahead(e, k)
                for k in range(UNITS - 2):
                    ahead(E - 1, k)
                if n == 0:
                    sp.wait_ge(s.eotok_free, 1 + E)
                    sp.dma_start(raw_g1[:, :, :], wg1T.rearrange("(c p) r -> p c r", p=P)).then_inc(g_raw_in, 16)
                    sp.dma_start(raw_g2[:, :], wg2T).then_inc(g_raw_in, 16)
            for g in range(GROUPS):
                sp.wait_ge(out_ready, g + 1)
                sp.dma_start(out_tiles[:, g * GROUP:(g + 1) * GROUP, :],
                             xt[:, g * GROUP:(g + 1) * GROUP, :]).then_inc(out_done, 16)
            sp.wait_ge(out_done, 16 * GROUPS)

        @block.gpsimd
        def _(pool):
            pool.memset(ident[:, :], 0.0).then_inc(pool_const, 1)
            pool.memset(tri[:, :], 1.0).then_inc(pool_const, 1)
            pool.memset(ones[:, :], 1.0).then_inc(pool_const, 1)
            pool.memset(expo[:, :], -0.5).then_inc(pool_const, 1)
            pool.wait_ge(pool_const, 4)
            pool.affine_select(out=ident[:, :], in_=ident[:, :], compare_op=ALU.not_equal, fill=1.0,
                               base=0, pattern=[[-1, P]], channel_multiplier=1).then_inc(pool_const, 1)
            pool.affine_select(out=tri[:, :], in_=tri[:, :], compare_op=ALU.is_ge, fill=0.0,
                               base=0, pattern=[[1, P]], channel_multiplier=-1).then_inc(pool_const, 1)
            pool.iota(desc[:, :, :], [[-1, E], [0, GROUP]], base=E, channel_multiplier=0,
                      allow_small_or_imprecise_dtypes=True).then_inc(pool_const, 1)
            pool.iota(slot0[:, :, :], [[CAP, E], [0, GROUP]], base=-1, channel_multiplier=0,
                      allow_small_or_imprecise_dtypes=True).then_inc(pool_const, 1)
            pool.iota(spare[:, :], [[P, TILES]], base=SLOTS, channel_multiplier=1,
                      allow_small_or_imprecise_dtypes=True).then_inc(pool_const, 1)

            def power(g, var_sem, rstd_sem):
                pool.wait_ge(var_sem, g + 1)
                q = slice(g * GROUP, (g + 1) * GROUP)
                pool.tensor_tensor(rstd[:, q], var[:, q], expo[:, q], ALU.pow).then_inc(rstd_sem, 1)
                pool.wait_ge(rstd_sem, 2 * g + 1)
                pool.tensor_tensor(shift[:, q], neg_mean[:, q], rstd[:, q], ALU.mult).then_inc(rstd_sem, 1)

            def scatter(g, s):
                pool.wait_ge(s.rows_done, g + 1)
                if s is layers[0] and g == 0:
                    pool.wait_ge(zero_out, 64)
                for t in range(g * GROUP, (g + 1) * GROUP):
                    pool.indirect_dma_start(disp[:, :], bass.IndirectOffsetOnAxis(ap=to_row[:, t:t + 1], axis=0),
                                            xn[:, t, :], None).then_inc(s.scattered, 16)

            def load_tokens(s, e):
                pool.dma_start(dtok[:, 0:2, :], disp[bass.ds(e * CAP, 256), :]
                               .rearrange("(c p) d -> p c d", p=P)).then_inc(s.dtok_in, 16)
                pool.dma_start(dtok[0:64, 2, :], disp[bass.ds(e * CAP + 256, 64), :]).then_inc(s.dtok_in, 16)

            for n, s in enumerate(layers):
                pool.sem_inc(s.eotok_free, 1)
                if n == 0:
                    power(0, s.var_done, s.rstd_done)
                    power(1, s.var_done, s.rstd_done)
                    for g in range(GROUPS):
                        if g + 2 < GROUPS:
                            power(g + 2, s.var_done, s.rstd_done)
                        scatter(g, s)
                else:
                    power(0, n_var, n_rstd)
                    for g in range(GROUPS + 2):
                        if g + 1 < GROUPS:
                            power(g + 1, n_var, n_rstd)
                        if g >= 2:
                            power(g - 2, s.var_done, s.rstd_done)
                    for g in range(GROUPS):
                        scatter(g, s)
                pool.wait_ge(s.scattered, 16 * TILES)
                load_tokens(s, 0)

                def expert(e, last, s=s):
                    pool.wait_ge(s.tokT_done, DC * e + DC)
                    load_tokens(s, 0 if last else e + 1)
                    pool.wait_ge(s.out_act, 1 + 2 * e + 2)
                    pool.wait_ge(s.out_dve, e + 1)
                    pool.dma_start(eout[bass.ds(e * CAP, 256), :].rearrange("(c p) d -> p c d", p=P),
                                   eotok[:, 0:2, :]).then_inc(s.eout_out, 16)
                    pool.dma_start(eout[bass.ds(e * CAP + 256, 64), :], eotok[0:64, 2, :]).then_inc(s.eout_out, 16)
                    pool.wait_ge(s.eout_out, 32 * e + 32)
                    pool.sem_inc(s.eotok_free, 1)

                with pool.Fori(0, E - 1) as e:
                    expert(e, False)
                expert(E - 1, True)
                if n == 0:
                    for c in (0, SEQ + 1):
                        pool.memset(xT[:, :, c:c + 1], 0.0).then_inc(n_pad, 1)
                for t in range(TILES):
                    pool.indirect_dma_start(xn[:, t, :], None, eout[:, :],
                                            bass.IndirectOffsetOnAxis(ap=from_row[:, t:t + 1], axis=0)
                                            ).then_inc(s.y_in[t // GROUP], 16)

        @block.scalar
        def _(act):
            copy = ACT.Copy
            for n, s in enumerate(layers):
                if n == 0:
                    for k, w in enumerate((wu, wv)):
                        act.wait_ge(uv_raw_in[k], 16)
                        act.activation(w[0][:, :, :], raw_wi[k][:, :, :], copy).then_inc(uv_hi, 1)
                act.sem_inc(s.gelu_done, ICS)
                act.sem_inc(s.eoT_done, 1)
                act.sem_inc(s.out_act, 1)
                for t in range(TILES):
                    act.wait_ge(s.xT_done, t + 1)
                    if t >= 2:
                        act.wait_ge(s.logits_done, t - 1)
                    act.activation(xTt[:, t % 2, :, :], psT[t % 2][:, :].rearrange("p (c q) -> p c q", c=DC),
                                   copy).then_inc(s.xT_copied, 1)
                    g = (t - 3) // GROUP
                    if t >= 7 and t % GROUP == 3:
                        act.wait_ge(s.diff_done, g)
                        act.activation(sel[:, (g - 1) % 2], sel[:, (g - 1) % 2], ACT.Exp).then_inc(s.exp_done, 1)
                act.wait_ge(s.diff_done, GROUPS)
                act.activation(sel[:, (GROUPS - 1) % 2], sel[:, (GROUPS - 1) % 2], ACT.Exp).then_inc(s.exp_done, 1)
                act.preload_act_table(ACT.Gelu)

                def wi_split(e, step, s=s):
                    k = (step // 2) % 2
                    if step % 2 == 0:
                        act.wait_ge(s.wi_in[k], 32 * e + 16 * (step // 4 + 1))
                    act.wait_ge(s.h_ready, ICS * STEPS * e + ICS * (step + 1))
                    act.activation(wih[:, step % 2, :, :],
                                   raw_wi[k][:, :, (step % 2) * HALF:(step % 2 + 1) * HALF],
                                   copy).then_inc(s.wi_hi, 1)

                def wo_split(e, step, s=s):
                    k = (step // 2) % 2
                    if step % 2 == 0:
                        act.wait_ge(s.wo_in[k], 32 * e + 16 * (step // 4 + 1))
                    act.wait_ge(s.mm2_done, STEPS * e + step + 1)
                    act.activation(woh[:, step % 2, :, :],
                                   raw_wo[k][:, (step % 2) * ICS:(step % 2 + 1) * ICS, :],
                                   copy).then_inc(s.wo_hi, 1)

                def tokens(e, c, s=s):
                    act.wait_ge(s.tokT_done, DC * e + c + 1)
                    act.activation(dth[:, c, :], psT[c % 2][:, 0:CAP], copy).then_inc(s.dt_hi, 1)

                wi_split(0, 0)
                wi_split(0, 1)
                wo_split(0, 0)
                for c in range(DC):
                    tokens(0, c)

                def expert(e, last, s=s):
                    for step in range(STEPS):
                        act.wait_ge(s.ht_lo, STEPS * e + step + 1)
                        for j in range(ICS):
                            ic = ICS * step + j
                            act.wait_ge(s.h_ready, 2 * ICS + ICS * STEPS * e + ic + 1)
                            act.activation(gel[:, step % 2, j, :], psH[j][:, 0:CAP],
                                           ACT.Gelu).then_inc(s.gelu_done, 1)
                        if step == STEPS - 1:
                            tokens(e + 1, 0)
                            tokens(e + 1, 1)
                        if not last or step + 2 < STEPS:
                            wi_split(e, step + 2)
                        if step == STEPS - 1:
                            tokens(e + 1, 2)
                            tokens(e + 1, 3)
                        if not last or step + 1 < STEPS:
                            wo_split(e, step + 1)
                    for c in range(DC):
                        act.wait_ge(s.acc_done, DC * e + c + 1)
                        act.activation(eoT[:, c, :], acc[c][:, 0:CAP], copy).then_inc(s.eoT_done, 1)
                    act.wait_ge(s.eotok_free, e + 1)
                    act.wait_ge(s.outT_done, 3 * e + 1)
                    act.activation(eotok[:, 0, :], psT[0][:, :], copy).then_inc(s.out_act, 1)
                    act.wait_ge(s.outT_done, 3 * e + 3)
                    act.activation(eotok[0:64, 2, :], psH[1][0:64, :], copy).then_inc(s.out_act, 1)

                with act.Fori(0, E - 1) as e:
                    expert(e, False)
                expert(E - 1, True)

                if n == 1:
                    break
                nxt = layers[1]
                act.wait_ge(g_raw_in, 32)
                act.activation(wg1[0][:, :, :], raw_g1[:, :, :], copy).then_inc(g_hi, 1)
                act.activation(wg2[0][:, :], raw_g2[:, :], copy).then_inc(g_hi, 1)

                def place(g):
                    return 1 + (g % 2) * GT

                def apply_norm(g, rstd_sem, xn_sem):
                    act.wait_ge(rstd_sem, 2 * (g + 1))
                    for t in range(g * GROUP, (g + 1) * GROUP):
                        ins = act.activation(xn[:, t, :], xt[:, t, :], ACT.Identity,
                                             bias=shift[:, t:t + 1], scale=rstd[:, t:t + 1])
                    ins.then_inc(xn_sem, 1)

                def copy_xT(g):
                    if g == 2:
                        act.wait_ge(d_tap, 2 * DC)
                    if g == 3:
                        act.wait_ge(d_conv, 2 * DC)
                    for c in range(DC):
                        act.wait_ge(n_T, DC * g + c + 1)
                        act.activation(xT[:, c, place(g):place(g) + GT], psT[c % 2][:, :], copy).then_inc(n_xT, 1)

                def split_xT(g):
                    act.wait_ge(n_xT, DC * (g + 1))
                    if g >= 2:
                        act.wait_ge(p_ring, RING * (g - 1))
                    for c in range(DC):
                        act.activation(xTh[:, g % 2, c, :], xT[:, c, place(g):place(g) + GT],
                                       copy).then_inc(n_xTh, 1)

                def conv_mid(g):
                    if g == 0:
                        act.wait_ge(g_lo, 2)
                    else:
                        act.wait_ge(p_conv, GROUP * g)
                    for c in range(DC):
                        act.activation(convT[:, c, :], xT[:, c, place(g):place(g) + GT], ACT.Identity,
                                       bias=small[:, CB0 + c:CB0 + c + 1],
                                       scale=small[:, CW0 + 3 * c + 1:CW0 + 3 * c + 2]).then_inc(a_conv, 1)

                def relu(g):
                    act.wait_ge(p_ring, RING * g + 1)
                    if g >= 1:
                        act.wait_ge(d_glob, DC * g)
                    act.activation(ug[:, :], acc[(RING * g) % 4][:, :], ACT.Relu,
                                   bias=small[:, BG10:BG10 + 1]).then_inc(a_h, 1)

                def glob_hi(i):
                    g, c = divmod(i, DC)
                    act.wait_ge(d_glob, i + 1)
                    if g >= 2:
                        act.wait_ge(p_uv, GROUP * (g - 1))
                    act.activation(glh[:, g % 2, c, :], vg[c % 2][:, :], copy).then_inc(a_glh, 1)

                apply_norm(0, n_rstd, n_xn)
                copy_xT(0)
                split_xT(0)
                relu(0)
                for g in range(GROUPS):
                    for c in range(DC):
                        i = DC * g + c
                        u = RING * g + 1 + 3 * c
                        if c == 3 and g + 1 < GROUPS:
                            copy_xT(g + 1)
                        act.wait_ge(p_ring, u + 1)
                        if i >= 1:
                            act.wait_ge(d_vg, i)
                        act.activation(gate[:, :], acc[u % 4][:, :], ACT.Sigmoid,
                                       bias=small[:, BG20 + c:BG20 + c + 1]).then_inc(a_gate, 1)
                        if c >= 1:
                            glob_hi(i - 1)
                        if c == 1:
                            conv_mid(g)
                        if c == 2 and g + 1 < GROUPS:
                            apply_norm(g + 1, n_rstd, n_xn)
                    if g + 1 < GROUPS:
                        split_xT(g + 1)
                        relu(g + 1)
                    glob_hi(DC * g + DC - 1)
                    if g >= 2:
                        apply_norm(g - 2, nxt.rstd_done, nxt.xn_done)
                for g in range(GROUPS - 2, GROUPS):
                    apply_norm(g, nxt.rstd_done, nxt.xn_done)

        @block.vector
        def _(dve):
            seq = [0]

            def then(ins):
                ins.then_inc(dve_seq, 1)
                seq[0] += 1

            def settle():
                dve.wait_ge(dve_seq, seq[0])

            def lo(out, full, hi):
                return dve.tensor_tensor(out, full, hi.bitcast(F32), ALU.subtract)

            def moments(g, var_sem):
                q = slice(g * GROUP, (g + 1) * GROUP)
                for j in range(GROUP):
                    then(dve.bn_stats(stats[:, j, :], xt[:, g * GROUP + j, :]))
                settle()
                for j in range(GROUP):
                    then(dve.bn_aggr(mv[:, g * GROUP + j, :], stats[:, j, :]))
                settle()
                then(dve.tensor_scalar(neg_mean[:, q], mv[:, q, 0], -1.0, None, ALU.mult))
                settle()
                dve.tensor_scalar(var[:, q], mv[:, q, 1], EPS, None, ALU.add).then_inc(var_sem, 1)

            def apply_norm(g, rstd_sem, xn_sem):
                dve.wait_ge(rstd_sem, 2 * g + 1)
                for t in range(g * GROUP, (g + 1) * GROUP):
                    ins = dve.tensor_scalar(xn[:, t, :], xt[:, t, :], mv[:, t, 0:1], rstd[:, t:t + 1],
                                            ALU.subtract, ALU.mult)
                ins.then_inc(xn_sem, 1)

            def add_ffn(g, s):
                dve.wait_ge(s.y_in[g], 16 * GROUP)
                for j in range(GROUP):
                    t = g * GROUP + j
                    ins = dve.scalar_tensor_tensor(xt[:, t, :], xn[:, t, :], weight[:, t:t + 1], xt[:, t, :],
                                                   ALU.mult, ALU.add)
                    if s is layers[0]:
                        then(ins)
                return ins

            def rows(g, s):
                by_t = "p e t -> p t e"
                q = slice(g * GROUP, (g + 1) * GROUP)
                a = g % 2

                def over(k):
                    return t4[:, k:k + 1, :].to_broadcast(each)

                dve.wait_ge(s.logits_done, GROUP * (g + 1))
                dve.tensor_copy(lg[:, :, :], ps_logit[a].rearrange("p (t e) -> p e t", e=E)
                                ).then_inc(s.lg_copied, 1)
                dve.wait_ge(s.lg_copied, g + 1)
                then(dve.tensor_reduce(t4[:, 0, :], lg[:, :, :].rearrange(by_t), AX_X, ALU.max))
                settle()
                dve.tensor_tensor(sel[:, a], lg[:, :, :], over(0), ALU.subtract).then_inc(s.diff_done, 1)
                then(dve.tensor_tensor(r8[:, :, :], lg[:, :, :], over(0), ALU.is_equal))
                settle()
                then(dve.tensor_tensor(r8[:, :, :], r8[:, :, :], desc[:, :, :], ALU.mult))
                settle()
                then(dve.tensor_reduce(t4[:, 1, :], r8[:, :, :].rearrange(by_t), AX_X, ALU.max))
                settle()
                dve.tensor_tensor(ohb[:, a], desc[:, :, :], over(1), ALU.is_equal).then_inc(s.oh_done, 1)
                dve.wait_ge(s.oh_done, g + 1)
                then(dve.tensor_tensor(r8[:, :, :], slot0[:, :, :], ohb[:, a], ALU.mult))
                then(dve.tensor_reduce(lg[:, :, 0], ohb[:, a], AX_X, ALU.add))
                settle()
                then(dve.tensor_reduce(t4[:, 5, :], r8[:, :, :].rearrange(by_t), AX_X, ALU.add))
                then(dve.tensor_tensor(so_far[:, :], so_far[:, :], lg[:, :, 0], ALU.add))
                settle()
                dve.tensor_copy(before[:, (g + 1) % 2, :], so_far[:, :]).then_inc(s.before_done, 1)
                dve.wait_ge(s.exp_done, g + 1)
                then(dve.tensor_reduce(t4[:, 2, :], sel[:, a].rearrange(by_t), AX_X, ALU.add))
                settle()
                then(dve.reciprocal(t4[:, 3, :], t4[:, 2, :]))
                dve.wait_ge(s.rank_done, g + 1)
                dve.tensor_tensor(r8[:, :, :], ps_rank[a].rearrange("p (e t) -> p e t", e=E), ohb[:, a],
                                  ALU.mult).then_inc(s.rank_used, 1)
                dve.wait_ge(s.rank_used, g + 1)
                then(dve.tensor_reduce(t4[:, 4, :], r8[:, :, :].rearrange(by_t), AX_X, ALU.add))
                settle()
                then(dve.tensor_scalar(t4[:, 6, :], t4[:, 4, :], float(CAP), None, ALU.is_le))
                then(dve.tensor_tensor(t4[:, 7, :], t4[:, 4, :], t4[:, 5, :], ALU.add))
                settle()
                then(dve.tensor_tensor(t4[:, 8, :], t4[:, 7, :], spare[:, q], ALU.subtract))
                then(dve.scalar_tensor_tensor(weight[:, q], t4[:, 3, :], 0.5, t4[:, 6, :], ALU.mult, ALU.mult))
                then(dve.tensor_tensor(from_row[:, q], t4[:, 7, :], t4[:, 6, :], ALU.mult))
                settle()
                then(dve.tensor_tensor(t4[:, 8, :], t4[:, 8, :], t4[:, 6, :], ALU.mult))
                settle()
                dve.tensor_tensor(to_row[:, q], t4[:, 8, :], spare[:, q], ALU.add).then_inc(s.rows_done, 1)

            def all_taken(s):
                dve.wait_ge(s.rank_done, GROUPS + 1)
                dve.tensor_copy(taken[:, :], ps_logit[0][:, 0:E]).then_inc(s.taken_done, 1)

            def start_count(s):
                then(dve.memset(so_far[:, :], 0.0))
                dve.memset(before[:, 0, :], 0.0).then_inc(s.before_done, 1)

            dve.memset(zeros[:, :], 0.0).then_inc(dve_const, 1)
            for bank in (*acc, *psH):
                then(dve.memset(bank[:, :], 0.0))
            then(dve.memset(one_col[:, :], 1.0))

            for n, s in enumerate(layers):
                dve.sem_inc(s.ht_lo, 2)
                start_count(s)
                if n == 0:
                    def first_norm(g):
                        dve.wait_ge(x_in[g], 16)
                        moments(g, s.var_done)
                        apply_norm(g, s.rstd_done, s.xn_done)

                    first_norm(0)
                    first_norm(1)
                    dve.wait_ge(pool_const, 9)
                    for g in range(GROUPS):
                        if g + 2 < GROUPS:
                            first_norm(g + 2)
                        rows(g, s)
                    all_taken(s)
                    for k, w in enumerate((wu, wv)):
                        dve.wait_ge(uv_hi, k + 1)
                        lo(w[1][:, :, :], raw_wi[k][:, :, :], w[0][:, :, :]).then_inc(uv_lo, 1)
                else:
                    for g in range(GROUPS):
                        rows(g, s)
                    all_taken(s)

                def wi_split(e, step, s=s):
                    k = (step // 2) % 2
                    dve.wait_ge(s.wi_hi, STEPS * e + step + 1)
                    lo(wil[:, step % 2, :, :], raw_wi[k][:, :, (step % 2) * HALF:(step % 2 + 1) * HALF],
                       wih[:, step % 2, :, :]).then_inc(s.wi_lo, 1)

                def wo_split(e, step, s=s):
                    k = (step // 2) % 2
                    dve.wait_ge(s.wo_hi, STEPS * e + step + 1)
                    lo(wol[:, step % 2, :, :], raw_wo[k][:, (step % 2) * ICS:(step % 2 + 1) * ICS, :],
                       woh[:, step % 2, :, :]).then_inc(s.wo_lo, 1)

                def tokens(e, c, s=s):
                    dve.wait_ge(s.dt_hi, DC * e + c + 1)
                    lo(dtl[:, c, :], psT[c % 2][:, 0:CAP], dth[:, c, :]).then_inc(s.dt_lo, 1)

                wi_split(0, 0)
                wi_split(0, 1)
                wo_split(0, 0)
                for c in range(DC):
                    tokens(0, c)

                def expert(e, last, s=s):
                    for step in range(STEPS):
                        k = step % 2
                        dve.wait_ge(s.gelu_done, ICS + ICS * (STEPS * e + step + 1))
                        dve.wait_ge(s.mm2_done, STEPS * e + step + 1)
                        dve.tensor_copy(hth[:, k, :, :], gel[:, k, :, :]).then_inc(s.ht_hi, 1)
                        dve.wait_ge(s.ht_hi, STEPS * e + step + 1)
                        lo(htl[:, k, :, :], gel[:, k, :, :], hth[:, k, :, :]).then_inc(s.ht_lo, 1)
                        if step == STEPS - 1:
                            tokens(e + 1, 0)
                            tokens(e + 1, 1)
                        if not last or step + 2 < STEPS:
                            wi_split(e, step + 2)
                        if step == STEPS - 1:
                            tokens(e + 1, 2)
                            tokens(e + 1, 3)
                        if not last or step + 1 < STEPS:
                            wo_split(e, step + 1)
                    dve.wait_ge(s.eotok_free, e + 1)
                    dve.wait_ge(s.outT_done, 3 * e + 2)
                    dve.tensor_copy(eotok[:, 1, :], psT[1][:, :]).then_inc(s.out_dve, 1)

                with dve.Fori(0, E - 1) as e:
                    expert(e, False)
                expert(E - 1, True)

                if n == 1:
                    for g in range(GROUPS):
                        add_ffn(g, s).then_inc(out_ready, 1)
                    break
                nxt = layers[1]

                def place(g):
                    return 1 + (g % 2) * GT

                def xT_lo(g):
                    for c in range(DC):
                        dve.wait_ge(n_xTh, DC * g + c + 1)
                        if c == 0 and g >= 2:
                            dve.wait_ge(p_ring, RING * (g - 1))
                        lo(xTl[:, g % 2, c, :], xT[:, c, place(g):place(g) + GT],
                           xTh[:, g % 2, c, :]).then_inc(n_xTl, 1)

                def split_h(g):
                    dve.wait_ge(a_h, g + 1)
                    dve.tensor_copy(hh[:, :], ug[:, :]).then_inc(d_hh, 1)
                    dve.wait_ge(d_hh, g + 1)
                    lo(hl[:, :], ug[:, :], hh[:, :]).then_inc(d_hl, 1)

                def glob_lo(i):
                    g, c = divmod(i, DC)
                    dve.wait_ge(a_glh, i + 1)
                    lo(gll[:, g % 2, c, :], vg[c % 2][:, :], glh[:, g % 2, c, :]).then_inc(d_gll, 1)

                def chain(g, c):
                    i = DC * g + c
                    u = RING * g + 1 + 3 * c
                    dve.wait_ge(a_gate, i + 1)
                    dve.wait_ge(p_ring, u + 2)
                    if c == 0:
                        dve.wait_ge(d_hl, g + 1)
                    else:
                        dve.wait_ge(d_glob, i)
                    dve.scalar_tensor_tensor(ug[:, :], acc[(u + 1) % 4][:, :], small[:, BU0 + c:BU0 + c + 1],
                                             gate[:, :], ALU.add, ALU.mult).then_inc(d_ug, 1)
                    if i >= 1:
                        glob_lo(i - 1)
                    dve.wait_ge(d_ug, i + 1)
                    start = 0.0 if g % 2 == 0 else carry[:, c:c + 1]
                    then(dve.tensor_tensor_scan(ug[:, :], one_col[:, :].to_broadcast([P, GT]), ug[:, :],
                                                start, ALU.mult, ALU.add))
                    dve.wait_ge(p_ring, u + 3)
                    dve.scalar_tensor_tensor(vg[c % 2][:, :], acc[(u + 2) % 4][:, :],
                                             small[:, BV0 + c:BV0 + c + 1],
                                             gate[:, :], ALU.add, ALU.mult).then_inc(d_vg, 1)
                    settle()
                    dve.wait_ge(d_vg, i + 1)
                    if g % 2 == 0:
                        then(dve.tensor_copy(carry[:, c:c + 1], ug[:, GT - 1:GT]))
                    dve.tensor_tensor(vg[c % 2][:, :], vg[c % 2][:, :], ug[:, :], ALU.mult).then_inc(d_glob, 1)

                def tap(g, k):
                    q = place(g) + k - 1
                    if k == 0:
                        dve.wait_ge(n_pad, 2)
                    else:
                        dve.wait_ge(n_xT, DC * (g + 2 - g % 2))
                    for c in range(DC):
                        dve.wait_ge(d_tap if k else a_conv, DC * g + c + 1)
                        dve.scalar_tensor_tensor(
                            convT[:, c, :], xT[:, c, q:q + GT],
                            small[:, CW0 + 3 * c + k:CW0 + 3 * c + k + 1], convT[:, c, :],
                            ALU.mult, ALU.add).then_inc(d_conv if k else d_tap, 1)

                def add_conv(g):
                    for w in range(GROUP * g, GROUP * (g + 1)):
                        dve.wait_ge(p_conv, w + 1)
                        dve.tensor_tensor(xt[:, w, :], psT[w % 2][:, :], xt[:, w, :], ALU.add).then_inc(d_addc, 1)

                def add_uv(w):
                    dve.wait_ge(p_uv, w + 1)
                    dve.wait_ge(d_addc, w + 1)
                    dve.tensor_tensor(xt[:, w, :], psH[w % 2][:, :], xt[:, w, :], ALU.add).then_inc(d_addu, 1)

                def next_moments(g):
                    dve.wait_ge(d_addu, GROUP * (g + 1))
                    moments(g, nxt.var_done)

                dve.wait_ge(g_hi, 2)
                lo(wg1[1][:, :, :], raw_g1[:, :, :], wg1[0][:, :, :]).then_inc(g_lo, 1)
                lo(wg2[1][:, :], raw_g2[:, :], wg2[0][:, :]).then_inc(g_lo, 1)
                add_ffn(0, s)
                settle()
                moments(0, n_var)
                xT_lo(0)
                split_h(0)
                for g in range(GROUPS):
                    more = g + 1 < GROUPS
                    for c in range(DC):
                        chain(g, c)
                        if c == 0:
                            if g >= 2:
                                add_uv(GROUP * (g - 2) + 3)
                            if more:
                                add_ffn(g + 1, s)
                            if g >= 1:
                                add_conv(g - 1)
                        elif g >= 1:
                            add_uv(GROUP * (g - 1) + c - 1)
                        if c == 1 and more:
                            settle()
                            moments(g + 1, n_var)
                        if c == 2:
                            tap(g, 0)
                            if g >= 2:
                                next_moments(g - 2)
                        if c == 3:
                            if more:
                                xT_lo(g + 1)
                                split_h(g + 1)
                            tap(g, 2)
                glob_lo(DC * GROUPS - 1)
                add_uv(GROUP * (GROUPS - 2) + 3)
                next_moments(GROUPS - 2)
                add_conv(GROUPS - 1)
                for j in range(GROUP):
                    add_uv(GROUP * (GROUPS - 1) + j)
                next_moments(GROUPS - 1)

        @block.tensor
        def _(pe):
            def product(out, lhs, rhs, first, last):
                (lh, ll), (rh, rl) = lhs, rhs
                pe.matmul(out, lh, rh, start=first, stop=False)
                pe.matmul(out, lh, rl, start=False, stop=False)
                return pe.matmul(out, ll, rh, start=False, stop=last)

            pe.wait_ge(pool_const, 9)
            for n, s in enumerate(layers):
                pe.sem_inc(s.h_ready, 2 * ICS)
                pe.sem_inc(s.mm2_done, 2)

                def turn(t, s=s):
                    pe.wait_ge(s.xn_done, t // GROUP + 1)
                    if t >= 2:
                        pe.wait_ge(s.xT_copied, t - 1)
                    for c in range(DC):
                        ins = pe.transpose(psT[t % 2][:, c * P:(c + 1) * P], xn[:, t, c * P:(c + 1) * P], ident[:, :])
                    ins.then_inc(s.xT_done, 1)

                def logits(t, s=s):
                    g, j = divmod(t, GROUP)
                    pe.wait_ge(s.xT_copied, t + 1)
                    if t == 0:
                        pe.wait_ge(small_loaded, 16)
                    if j == 0 and g >= 2:
                        pe.wait_ge(s.lg_copied, g - 1)
                    for c in range(DC):
                        ins = pe.matmul(ps_logit[g % 2][:, j * E:(j + 1) * E], xTt[:, t % 2, c, :],
                                        small[:, GATE0 + c * E:GATE0 + (c + 1) * E],
                                        start=(c == 0), stop=(c == DC - 1))
                    ins.then_inc(s.logits_done, 1)

                def ranks(g, s=s):
                    a = g % 2
                    out = ps_rank[a].rearrange("p (e t) -> p e t", e=E)
                    pe.wait_ge(s.oh_done, g + 1)
                    pe.wait_ge(s.before_done, g + 1)
                    if g >= 2:
                        pe.wait_ge(s.rank_used, g - 1)
                    pe.matmul(out, tri[:, :], ohb[:, a], start=True, stop=False)
                    for k in range(1, GROUP):
                        pe.matmul(out[:, :, k:], ones[:, :], ohb[:, a, :, 0:GROUP - k], start=False, stop=False)
                    pe.matmul(out, ones[:, :], before[:, a, :].unsqueeze(2).to_broadcast(each),
                              start=False, stop=True).then_inc(s.rank_done, 1)

                turn(0)
                for t in range(1, TILES):
                    turn(t)
                    logits(t - 1)
                    if t >= 7 and t % GROUP == 3:
                        ranks(t // GROUP - 1)
                logits(TILES - 1)
                ranks(GROUPS - 1)
                pe.wait_ge(s.before_done, GROUPS + 1)
                pe.wait_ge(s.lg_copied, GROUPS)
                pe.matmul(ps_logit[0][:, 0:E], ones[:, :], before[:, GROUPS % 2, :],
                          start=True, stop=True).then_inc(s.rank_done, 1)

                def turn_tokens(e, c, s=s):
                    pe.wait_ge(s.dtok_in, 32 * e + 32)
                    if c >= 2:
                        pe.wait_ge(s.dt_lo, DC * e + c - 1)
                    for k, (q, m) in enumerate(PARTS):
                        ins = pe.transpose(psT[c % 2][:, q:q + m], dtok[0:m, k, c * P:(c + 1) * P], ident[0:m, 0:m])
                    ins.then_inc(s.tokT_done, 1)

                def mm1(e, step, w, s=s):
                    k = step % 2
                    pe.wait_ge(s.wi_lo, STEPS * e + step + 1)
                    for j in range(ICS):
                        ic = ICS * step + j
                        if step > 0:
                            pe.wait_ge(s.gelu_done, ICS * STEPS * e + ic + 1)
                        if ic == 1:
                            pe.wait_ge(s.out_act, 1 + 2 * e)
                        for c in range(DC):
                            i = slice(j * P, (j + 1) * P)
                            ins = product(psH[j][:, 0:w], (wih[:, k, c, i], wil[:, k, c, i]),
                                          (dth[:, c, 0:w], dtl[:, c, 0:w]), c == 0, c == DC - 1)
                        ins.then_inc(s.h_ready, 1)

                def mm2(e, step, w, s=s):
                    k = step % 2
                    pe.wait_ge(s.wo_lo, STEPS * e + step + 1)
                    pe.wait_ge(s.ht_lo, 2 + STEPS * e + step + 1)
                    for c in range(DC):
                        for j in range(ICS):
                            d = slice(c * P, (c + 1) * P)
                            ins = product(acc[c][:, 0:w], (woh[:, k, j, d], wol[:, k, j, d]),
                                          (hth[:, k, j, 0:w], htl[:, k, j, 0:w]),
                                          step == 0 and j == 0, step == STEPS - 1 and j == ICS - 1)
                        if step == STEPS - 1 and c < DC - 1:
                            ins.then_inc(s.acc_done, 1)
                    return ins

                def turn_out(e, s=s):
                    banks = (psT[0], psT[1], psH[1])
                    pe.wait_ge(s.dt_lo, DC * (e + 1) + DC)
                    for c in range(DC):
                        pe.wait_ge(s.eoT_done, 1 + DC * e + c + 1)
                        for k, (q, m) in enumerate(PARTS):
                            ins = pe.transpose(banks[k][0:m, c * P:(c + 1) * P], eoT[:, c, q:q + m], ident[:, :])
                            if c == 0 and k == 0:
                                ins.then_inc(s.mm2_done, 1)
                            if c == DC - 1:
                                ins.then_inc(s.outT_done, 1)

                for c in range(DC):
                    turn_tokens(0, c)

                def expert(e, w):
                    mm1(e, 0, w)
                    for step in range(1, STEPS):
                        mm1(e, step, w)
                        if step == STEPS - 1:
                            turn_tokens(e + 1, 0)
                            turn_tokens(e + 1, 1)
                        mm2(e, step - 1, w).then_inc(s.mm2_done, 1)
                    turn_tokens(e + 1, 2)
                    turn_tokens(e + 1, 3)
                    mm2(e, STEPS - 1, w).then_inc(s.acc_done, 1)
                    turn_out(e)

                def at_width(e, tokens, widths):
                    if len(widths) == 1:
                        expert(e, widths[0])
                        return
                    with pe.If(tokens < widths[0] + 1):
                        expert(e, widths[0])
                    with pe.Else():
                        at_width(e, tokens, widths[1:])

                pe.wait_ge(s.taken_done, 1)
                pe.wait_ge(s.dt_lo, DC)
                with pe.Fori(0, E) as e:
                    at_width(e, pe.value_load(taken[0:1, bass.ds(e, 1)]), WIDTHS)

                if n == 1:
                    break
                used = [0]

                def bank():
                    u = used[0]
                    if u >= 4:
                        g, k = divmod(u - 4, RING)
                        if k == 0:
                            pe.wait_ge(a_h, g + 1)
                        else:
                            c, kind = divmod(k - 1, 3)
                            pe.wait_ge((a_gate, d_ug, d_vg)[kind], DC * g + c + 1)
                    used[0] += 1
                    return acc[u % 4][:, :]

                turned = []

                def turn_bank(freed_by, value):
                    k = len(turned)
                    if k >= 2:
                        pe.wait_ge(*turned[k - 2])
                    turned.append((freed_by, value))
                    return psT[k % 2]

                def turn_group(g):
                    pe.wait_ge(n_xn, g + 1)
                    for c in range(DC):
                        to = turn_bank(n_xT, DC * g + c + 1)
                        for j in range(GROUP):
                            ins = pe.transpose(to[:, j * P:(j + 1) * P],
                                               xn[:, GROUP * g + j, c * P:(c + 1) * P], ident[:, :])
                        ins.then_inc(n_T, 1)

                def turn_conv(g):
                    pe.wait_ge(d_conv, DC * (g + 1))
                    for j in range(GROUP):
                        to = turn_bank(d_addc, GROUP * g + j + 1)
                        for c in range(DC):
                            ins = pe.transpose(to[:, c * P:(c + 1) * P], convT[:, c, j * P:(j + 1) * P],
                                               ident[:, :])
                        ins.then_inc(p_conv, 1)

                def times_wu(g, j):
                    w = GROUP * g + j
                    a = g % 2
                    if j == 0:
                        pe.wait_ge(d_gll, DC * (g + 1))
                    if w >= 2:
                        pe.wait_ge(d_addu, w - 1)
                    q = slice(j * P, (j + 1) * P)
                    for c in range(DC):
                        ins = product(psH[j % 2][:, :], (glh[:, a, c, q], gll[:, a, c, q]),
                                      (wu[0][:, c, :], wu[1][:, c, :]), c == 0, c == DC - 1)
                    ins.then_inc(p_uv, 1)

                def hidden(g):
                    a = g % 2
                    pe.wait_ge(n_xTl, DC * (g + 1))
                    to = bank()
                    for c in range(DC):
                        ins = product(to, (wg1[0][:, c, :], wg1[1][:, c, :]), (xTh[:, a, c, :], xTl[:, a, c, :]),
                                      c == 0, c == DC - 1)
                    ins.then_inc(p_ring, 1)

                def projection(g, w, c):
                    a = g % 2
                    to = bank()
                    r = slice(c * P, (c + 1) * P)
                    for k in range(DC):
                        ins = product(to, (w[0][:, k, r], w[1][:, k, r]), (xTh[:, a, k, :], xTl[:, a, k, :]),
                                      k == 0, k == DC - 1)
                    ins.then_inc(p_ring, 1)

                turn_group(0)
                pe.wait_ge(g_lo, 2)
                pe.wait_ge(uv_lo, 2)
                hidden(0)
                for g in range(GROUPS):
                    for c in range(DC):
                        if c == 0:
                            pe.wait_ge(d_hl, g + 1)
                        to = bank()
                        r = slice(c * P, (c + 1) * P)
                        product(to, (wg2[0][:, r], wg2[1][:, r]), (hh[:, :], hl[:, :]), True, True).then_inc(p_ring, 1)
                        projection(g, wu, c)
                        projection(g, wv, c)
                        if g >= 1:
                            if c == 0:
                                turn_conv(g - 1)
                            times_wu(g - 1, c)
                        if c == 2 and g + 1 < GROUPS:
                            turn_group(g + 1)
                    if g + 1 < GROUPS:
                        hidden(g + 1)
                turn_conv(GROUPS - 1)
                for j in range(GROUP):
                    times_wu(GROUPS - 1, j)


def kernel(L0_attn_x, L0_attn_Wu, L0_attn_bu, L0_attn_Wv, L0_attn_bv, L0_attn_Wg1, L0_attn_bg1, L0_attn_Wg2,
           L0_attn_bg2, L0_attn_conv_w, L0_attn_conv_b, L0_ffn_gate_weight, L0_ffn_wi, L0_ffn_wo):
    import numpy as np
    import concourse.bacc as bacc
    from concourse.bass_utils import run_bass_kernel_spmd

    def cols(v):
        v = np.asarray(v).reshape(np.shape(v)[0] // P, P, -1)
        return v.transpose(1, 0, 2).reshape(P, -1)

    small = np.zeros((P, SMALL), np.float32)
    small[:, GATE0:BU0] = cols(np.asarray(L0_ffn_gate_weight).T)
    small[:, BU0:BV0] = cols(L0_attn_bu)
    small[:, BV0:BG20] = cols(L0_attn_bv)
    small[:, BG20:CB0] = cols(L0_attn_bg2)
    small[:, CB0:BG10] = cols(L0_attn_conv_b)
    small[:, BG10:CW0] = cols(L0_attn_bg1)
    small[:, CW0:CW0 + 3 * DC] = cols(np.asarray(L0_attn_conv_w)[:, 0, :])

    arrays = {
        "x": L0_attn_x,
        "wuT": np.asarray(L0_attn_Wu).T,
        "wvT": np.asarray(L0_attn_Wv).T,
        "wg1T": np.asarray(L0_attn_Wg1).T,
        "wg2T": np.asarray(L0_attn_Wg2).T,
        "small": small,
        "wi": L0_ffn_wi,
        "wo": L0_ffn_wo,
    }
    nc = bacc.Bacc("TRN2", target_bir_lowering=False, num_devices=1)
    sent, args = {}, []
    for name, a in arrays.items():
        a = np.ascontiguousarray(a)
        sent[f"in_{name}"] = a
        args.append(nc.dram_tensor(f"in_{name}", a.shape, mybir.dt.from_np(a.dtype), kind="ExternalInput").ap())
    out = nc.dram_tensor("out_x", (BATCH, SEQ, D), F32, kind="ExternalOutput").ap()
    build_kernel(nc, *args, out)
    return run_bass_kernel_spmd(nc, [sent], core_ids=[0]).results[0]["out_x"]
```

```python
from contextlib import ExitStack

import concourse.bass as bass
from concourse import mybir

ALU = mybir.AluOpType
ACT = mybir.ActivationFunctionType
F32 = mybir.dt.float32
F32R = mybir.dt.float32r
BF16 = mybir.dt.bfloat16
I32 = mybir.dt.int32
AX_X = mybir.AxisListType.X

P = 128
BATCH, SEQ, D = 2, 1024, 512
T = BATCH * SEQ
TILES = T // P
DC = D // P
E, INTER = 8, 2048
CAP = 320
SLOTS = E * CAP
PARTS = [(0, 128), (128, 128), (256, 64)]
WIDTHS = range(240, CAP + 1, 16)
GROUP = 4
GROUPS = TILES // GROUP
GT = GROUP * P
UNIT = 512
UNITS = INTER // UNIT
HALF = 256
STEPS = INTER // HALF
ICS = HALF // P
DH = D // 4
ROW = D + 4
W_COL, STD_COL, MEAN_COL, TOKEN_COL = range(D, ROW)
EPS = 1e-5
KB = 1024

GATE0, BU0, BV0, BG20, CB0, BG10, CW0, SMALL = 0, 32, 36, 40, 44, 48, 49, 64


def build_kernel(nc, x, wuT, wvT, wg1T, wg2T, small_in, wi, wo, out):
    x_tiles = x.rearrange("b (n p) d -> p (b n) d", p=P)
    out_tiles = out[0:T, :].rearrange("(n p) d -> p n d", p=P)
    disp = nc.dram_tensor("disp", [SLOTS + T, ROW], F32, kind="Internal").ap()
    x1 = nc.dram_tensor("x1", [T + SLOTS, D], F32, kind="Internal").ap()

    with ExitStack() as ctx:
        base = (nc.sbuf_base + 31) // 32 * 32
        top = [base]

        def at(name, shape, dt, offset):
            return nc.alloc_sbuf_tensor_at(name, shape, dt, offset=offset)

        def size(shape, dt):
            n = 2 if dt is BF16 else 4
            for s in shape[1:]:
                n *= s
            return (n + 31) // 32 * 32

        def put(name, shape, dt):
            t = at(name, shape, dt, top[0])
            top[0] += size(shape, dt)
            return t

        a_xt = top[0]
        xt = put("xt", [P, TILES, D], F32)
        a_xn = top[0]
        xn = put("xn", [P, TILES, ROW], F32)
        wu = [put(f"wu{k}", [P, DC, D], F32R) for k in "hl"]
        wv = [put(f"wv{k}", [P, DC, D], F32R) for k in "hl"]
        wg1 = [put(f"wg1{k}", [P, DC, DH], F32R) for k in "hl"]
        wg2 = [put(f"wg2{k}", [P, D], F32R) for k in "hl"]
        ident = put("ident", [P, P], F32)
        tri = put("tri", [P, P], BF16)
        ones = put("ones", [P, P], BF16)
        desc = put("desc", [P, E, GROUP], F32)
        slot0 = put("slot0", [P, E, GROUP], F32)
        spare = put("spare", [P, TILES], F32)
        small = put("small", [P, SMALL], F32)
        expo = put("expo", [P, TILES], F32)
        mv = put("mv", [P, TILES, 2], F32)
        var = put("var", [P, TILES], F32)
        rstd = put("rstd", [P, TILES], F32)
        neg_mean = put("neg_mean", [P, TILES], F32)
        shift = put("shift", [P, TILES], F32)
        to_row = put("to_row", [P, TILES], I32)
        taken = put("taken", [P, E + 1], I32)
        slot_rows = put("slot_rows", [P, SLOTS // P], F32)
        res_row = put("res_row", [P, len(PARTS)], I32)
        slot_w = put("slot_w", [P, len(PARTS)], F32)
        carry = put("carry", [P, DC], F32)
        stats = put("stats", [P, GROUP, 6], F32)
        one_col = put("one_col", [P, 1], F32)

        shared = top[0]
        raw_wi = [put(f"raw_wi{k}", [P, DC, UNIT], F32) for k in range(2)]
        raw_wo = [put(f"raw_wo{k}", [P, DC, UNIT], F32) for k in range(2)]
        wih = put("wih", [P, 2, DC, HALF], F32R)
        wil = put("wil", [P, 2, DC, HALF], F32R)
        woh = put("woh", [P, 2, ICS, D], F32R)
        wol = put("wol", [P, 2, ICS, D], F32R)
        a_gel = top[0]
        gel = put("gel", [P, 2, ICS, CAP], F32)
        hth = put("hth", [P, 2, ICS, CAP], F32R)
        htl = put("htl", [P, 2, ICS, CAP], F32R)
        dth = put("dth", [P, DC, CAP], F32R)
        dtl = put("dtl", [P, DC, CAP], F32R)
        dtok = put("dtok", [P, len(PARTS), ROW], F32)
        eoT = put("eoT", [P, DC, CAP], F32)
        ffn_top = top[0]
        top[0] = a_gel
        zeros = put("zeros", [P, SLOTS // P // 4 * TOKEN_COL], F32)
        xr = at("xr", [P, len(PARTS), D], F32, a_xn)
        eotok = at("eotok", [P, len(PARTS), D], F32, a_xn + size(xr.shape, F32))
        raw_u = [at(f"raw_u{k}", [P, DC, D], F32, a_xt + 8 * KB * k) for k in range(2)]
        raw_g1 = at("raw_g1", [P, DC, DH], F32, a_xt + 16 * KB)
        raw_g2 = at("raw_g2", [P, D], F32, a_xt + 18 * KB)
        top[0] = shared
        xT = put("xT", [P, DC, SEQ + 2], F32)
        glh = put("glh", [P, 2, DC, GT], F32R)
        a_xTt = top[0]
        assert a_xTt >= shared + 32 * KB
        xTh = [put("xTh0", [P, DC, GT], F32R)]
        xTl = [put("xTl0", [P, DC, GT], F32R)]
        xTh += [put("xTh1", [P, DC, GT], F32R)]
        xTl += [put("xTl1", [P, DC, GT], F32R)]
        gll = put("gll", [P, 2, DC, GT], F32R)
        hid = put("hid", [P, GT], F32)
        hh = put("hh", [P, GT], F32R)
        hl = put("hl", [P, GT], F32R)
        gate = put("gate", [P, GT], F32)
        ug = put("ug", [P, GT], F32)
        vg = [put(f"vg{k}", [P, GT], F32) for k in range(2)]
        xTt = at("xTt", [P, 2, DC, GT], F32, a_xTt)
        lgT = put("lgT", [E, GT], F32)
        each = [P, E, GROUP]
        lg = put("lg", each, F32)
        sel = put("sel", [P, 2, E, GROUP], F32)
        ohb = put("ohb", [P, 2, E, GROUP], BF16)
        r8 = put("r8", [P, 2, E, GROUP], F32)
        t4 = put("t4", [P, 2, 9, GROUP], F32)
        before = put("before", [P, GROUPS + 1, E], BF16)
        so_far = put("so_far", [P, E], F32)
        assert max(top[0], ffn_top) <= nc.sbuf_usable_end, (top[0], ffn_top, nc.sbuf_usable_end)

        acc = [ctx.enter_context(nc.psum_tensor(f"acc{k}", [P, 512], F32)) for k in range(4)]
        psH = [ctx.enter_context(nc.psum_tensor(f"psH{k}", [P, 512], F32)) for k in range(2)]
        psT = [ctx.enter_context(nc.psum_tensor(f"psT{k}", [P, 512], F32)) for k in range(2)]
        ps_logitT = [acc[k][0:E, :] for k in (0, 1)]
        ps_logit = [acc[k][:, 0:GROUP * E] for k in (0, 1)]
        ps_rank = [acc[k][:, 0:GROUP * E] for k in (2, 3)]

        def sem(name):
            return ctx.enter_context(nc.semaphore(name))

        class Layer:

            def __init__(self, n):
                self.var_done = sem(f"var_done{n}")
                self.rstd_done = sem(f"rstd_done{n}")
                self.xn_done = sem(f"xn_done{n}")
                self.xn_done0 = sem(f"xn_done0_{n}")
                self.cols_done = sem(f"cols_done{n}")
                self.slots_set = sem(f"slots_set{n}")
                self.xT_done = sem(f"xT_done{n}")
                self.xT_copied = sem(f"xT_copied{n}")
                self.logits_done = sem(f"logits_done{n}")
                self.lgT_copied = sem(f"lgT_copied{n}")
                self.lg_turned = sem(f"lg_turned{n}")
                self.lg_copied = sem(f"lg_copied{n}")
                self.diff_done = sem(f"diff_done{n}")
                self.exp_done = sem(f"exp_done{n}")
                self.oh_done = sem(f"oh_done{n}")
                self.before_done = sem(f"before_done{n}")
                self.rank_done = sem(f"rank_done{n}")
                self.rank_used = sem(f"rank_used{n}")
                self.taken_done = sem(f"taken_done{n}")
                self.rows_done = sem(f"rows_done{n}")
                self.scattered = sem(f"scattered{n}")
                self.wi_in = [sem(f"wi_in{n}_{k}") for k in range(2)]
                self.wo_in = [sem(f"wo_in{n}_{k}") for k in range(2)]
                self.wi_hi = sem(f"wi_hi{n}")
                self.wi_lo = sem(f"wi_lo{n}")
                self.wo_hi = sem(f"wo_hi{n}")
                self.wo_lo = sem(f"wo_lo{n}")
                self.h_ready = sem(f"h_ready{n}")
                self.gelu_done = sem(f"gelu_done{n}")
                self.ht_hi = sem(f"ht_hi{n}")
                self.ht_lo = sem(f"ht_lo{n}")
                self.mm2_done = sem(f"mm2_done{n}")
                self.acc_done = sem(f"acc_done{n}")
                self.eoT_done = sem(f"eoT_done{n}")
                self.dtok_in = sem(f"dtok_in{n}")
                self.tokT_done = sem(f"tokT_done{n}")
                self.dt_hi = sem(f"dt_hi{n}")
                self.dt_lo = sem(f"dt_lo{n}")
                self.outT_done = sem(f"outT_done{n}")
                self.rows_set = sem(f"rows_set{n}")
                self.meta = sem(f"meta{n}")
                self.may_send = sem(f"may_send{n}")
                self.xr_done = sem(f"xr_done{n}")
                self.out_dve = sem(f"out_dve{n}")
                self.kept = sem(f"kept{n}")
                self.res_out = sem(f"res_out{n}")
                self.eotok_free = sem(f"eotok_free{n}")

        layers = [Layer(0), Layer(1)]
        x_tile = [sem(f"x_tile{j}") for j in range(GROUP)]
        x_in = [sem(f"x_in{g}") for g in range(1, GROUPS)]
        small_loaded = sem("small_loaded")
        w_raw_in = sem("w_raw_in")
        uv_hi = sem("uv_hi")
        uv_lo = sem("uv_lo")
        g_hi = sem("g_hi")
        g_lo = sem("g_lo")
        pool_const = sem("pool_const")
        dve_const = sem("dve_const")
        zero_out = sem("zero_out")
        dve_seq = sem("dve_seq")
        x1_tile = [sem(f"x1_tile{j}") for j in range(GROUP)]
        x1_in = [sem(f"x1_in{g}") for g in range(1, GROUPS)]
        n_xn0 = sem("n_xn0")
        n_var = sem("n_var")
        n_rstd = sem("n_rstd")
        n_xn = sem("n_xn")
        n_T = sem("n_T")
        n_xT = sem("n_xT")
        n_pad = sem("n_pad")
        n_xTh = sem("n_xTh")
        n_xTl = sem("n_xTl")
        p_ring = sem("p_ring")
        a_h = sem("a_h")
        d_hh = sem("d_hh")
        d_hl = sem("d_hl")
        a_gate = sem("a_gate")
        d_ug = sem("d_ug")
        d_vg = sem("d_vg")
        d_glob = sem("d_glob")
        a_glh = sem("a_glh")
        d_gll = sem("d_gll")
        a_conv = sem("a_conv")
        d_tap = sem("d_tap")
        d_conv = sem("d_conv")
        p_conv = sem("p_conv")
        d_addc = sem("d_addc")
        p_uv = sem("p_uv")
        d_addu = sem("d_addu")
        block = ctx.enter_context(nc.Block())

        FIRST = (psT[0], psT[1], acc[2], acc[3])
        HELD = [(0, psT[0]), (2, psH[1]), (1, psT[1])]
        RING = 1 + 3 * DC

        def i_gate(g, c):
            return 1 + RING * g + 3 * c

        def i_u(g, c):
            return i_gate(g, c) + 1

        def i_v(g, c):
            return i_gate(g, c) + (3 if c == DC - 1 and g < GROUPS - 1 else 2)

        def i_h(g):
            return i_u(g - 1, DC - 1) + 1 if g else 0

        def convT(g, c):
            return xn[:, GROUP * g + c, 0:D]

        @block.sync
        def _(sp):
            sp.dma_start(small[:, :], small_in).then_inc(small_loaded, 16)
            for j in range(GROUP):
                sp.dma_start(xt[:, j, :], x_tiles[:, j, :]).then_inc(x_tile[j], 16)
            for g in range(1, GROUPS):
                sp.dma_start(xt[:, g * GROUP:(g + 1) * GROUP, :],
                             x_tiles[:, g * GROUP:(g + 1) * GROUP, :]).then_inc(x_in[g - 1], 16)
            sp.wait_ge(dve_const, 1)
            for k in range(4):
                rows = SLOTS // 4
                sp.dma_start(disp[k * rows:(k + 1) * rows, 0:TOKEN_COL].rearrange("(p r) d -> p r d", p=P),
                             zeros[:, :].rearrange("p (r d) -> p r d", d=TOKEN_COL)).then_inc(zero_out, 16)

            def load_wi(s, e, u, k):
                sp.dma_start(raw_wi[k][:, :, :],
                             wi[bass.ds(e, 1), :, u * UNIT:(u + 1) * UNIT]
                             .rearrange("a (c p) i -> p (a c) i", p=P)).then_inc(s.wi_in[k], 16)

            def load_wo(s, e, u, k):
                sp.dma_start(raw_wo[k][:, :, :],
                             wo[bass.ds(e, 1), u * UNIT:(u + 1) * UNIT, :]
                             .rearrange("a (c p) d -> p (a c) d", p=P)).then_inc(s.wo_in[k], 16)

            def load_tokens(s, e):
                sp.dma_start(dtok[:, 0:2, :], disp[bass.ds(e * CAP, 256), :]
                             .rearrange("(c p) d -> p c d", p=P)).then_inc(s.dtok_in, 16)
                sp.dma_start(dtok[0:64, 2, :], disp[bass.ds(e * CAP + 256, 64), :]).then_inc(s.dtok_in, 16)

            for n, s in enumerate(layers):
                if n == 1:
                    for g in range(GROUPS - 1):
                        sp.wait_ge(d_addu, GROUP * (g + 1))
                        q = slice(g * GROUP, (g + 1) * GROUP)
                        sp.dma_start(out_tiles[:, q, :], xt[:, q, :]).then_inc(s.kept, 16)
                    sp.wait_ge(d_addu, TILES)
                for k in range(2):
                    load_wi(s, 0, k, k)
                sp.wait_ge(s.scattered, 16 * TILES)
                sp.wait_ge(s.taken_done, 1)
                load_tokens(s, 0)
                for k in range(2):
                    load_wo(s, 0, k, k)
                if n == 1:
                    q = slice((GROUPS - 1) * GROUP, TILES)
                    sp.dma_start(out_tiles[:, q, :], xt[:, q, :]).then_inc(s.kept, 16)

                def next_tokens(e, following, s=s):
                    sp.wait_ge(s.tokT_done, DC * e + DC)
                    sp.wait_ge(s.xr_done, 3 * e + 3)
                    sp.wait_ge(s.meta, 4 * e + 4)
                    load_tokens(s, following)

                def ahead(e, k, s=s):
                    if k == 2:
                        next_tokens(e, e + 1)
                    done = e * STEPS + 2 * (k + 1)
                    sp.wait_ge(s.wi_lo, done)
                    load_wi(s, e + (k + 2) // UNITS, (k + 2) % UNITS, k % 2)
                    sp.wait_ge(s.wo_lo, done)
                    load_wo(s, e + (k + 2) // UNITS, (k + 2) % UNITS, k % 2)

                for k in range(UNITS):
                    ahead(0, k)
                    if n == 0:
                        q = slice(k * T // UNITS, (k + 1) * T // UNITS)
                        sp.dma_start(x1[q, :], x.rearrange("b l d -> (b l) d")[q, :]).then_inc(s.kept, 16)
                if n == 0:
                    sp.wait_ge(s.xn_done, GROUPS)
                    sp.wait_ge(s.xn_done0, 1)
                    sp.dma_start(raw_u[0][:, :, :], wuT.rearrange("(c p) r -> p c r", p=P)).then_inc(w_raw_in, 16)
                    sp.dma_start(raw_u[1][:, :, :], wvT.rearrange("(c p) r -> p c r", p=P)).then_inc(w_raw_in, 16)
                    sp.dma_start(raw_g1[:, :, :], wg1T.rearrange("(c p) r -> p c r", p=P)).then_inc(w_raw_in, 16)
                    sp.dma_start(raw_g2[:, :], wg2T).then_inc(w_raw_in, 16)

                with sp.Fori(1, E - 1) as e:
                    for k in range(UNITS):
                        ahead(e, k)
                for k in range(UNITS - 2):
                    ahead(E - 1, k)
                next_tokens(E - 1, 0)
                if n == 0:
                    sp.wait_ge(uv_lo, 2 * DC)
                    sp.wait_ge(g_lo, 2)
                    sp.wait_ge(s.res_out, 48 * E)
                    x1_tiles = x1[0:T, :].rearrange("(n p) d -> p n d", p=P)
                    for j in range(GROUP):
                        sp.dma_start(xt[:, j, :], x1_tiles[:, j, :]).then_inc(x1_tile[j], 16)
                    for g in range(1, GROUPS):
                        q = slice(g * GROUP, (g + 1) * GROUP)
                        sp.dma_start(xt[:, q, :], x1_tiles[:, q, :]).then_inc(x1_in[g - 1], 16)
            sp.wait_ge(layers[1].res_out, 48 * E)

        @block.gpsimd
        def _(pool):
            pool.memset(ident[:, :], 0.0).then_inc(pool_const, 1)
            pool.memset(tri[:, :], 1.0).then_inc(pool_const, 1)
            pool.memset(ones[:, :], 1.0).then_inc(pool_const, 1)
            pool.memset(expo[:, :], -0.5).then_inc(pool_const, 1)
            pool.wait_ge(pool_const, 4)
            pool.affine_select(out=ident[:, :], in_=ident[:, :], compare_op=ALU.not_equal, fill=1.0,
                               base=0, pattern=[[-1, P]], channel_multiplier=1).then_inc(pool_const, 1)
            pool.affine_select(out=tri[:, :], in_=tri[:, :], compare_op=ALU.is_ge, fill=0.0,
                               base=0, pattern=[[1, P]], channel_multiplier=-1).then_inc(pool_const, 1)
            pool.iota(desc[:, :, :], [[-1, E], [0, GROUP]], base=E, channel_multiplier=0,
                      allow_small_or_imprecise_dtypes=True).then_inc(pool_const, 1)
            pool.iota(slot0[:, :, :], [[CAP, E], [0, GROUP]], base=-1, channel_multiplier=0,
                      allow_small_or_imprecise_dtypes=True).then_inc(pool_const, 1)
            pool.iota(spare[:, :], [[P, TILES]], base=SLOTS, channel_multiplier=1,
                      allow_small_or_imprecise_dtypes=True).then_inc(pool_const, 1)
            pool.iota(slot_rows[:, :], [[1, SLOTS // P]], base=T, channel_multiplier=SLOTS // P,
                      allow_small_or_imprecise_dtypes=True).then_inc(pool_const, 1)

            def power(g, var_sem, rstd_sem):
                pool.wait_ge(var_sem, g + 1)
                q = slice(g * GROUP, (g + 1) * GROUP)
                pool.tensor_tensor(rstd[:, q], var[:, q], expo[:, q], ALU.pow).then_inc(rstd_sem, 1)
                pool.wait_ge(rstd_sem, 2 * g + 1)
                pool.tensor_tensor(shift[:, q], neg_mean[:, q], rstd[:, q], ALU.mult).then_inc(rstd_sem, 1)

            def columns(g, s):
                pool.wait_ge(s.rstd_done, 2 * g + 2)
                q = slice(g * GROUP, (g + 1) * GROUP)
                pool.tensor_tensor(xn[:, q, STD_COL], var[:, q], rstd[:, q], ALU.mult).then_inc(s.cols_done, 1)
                pool.tensor_copy(xn[:, q, MEAN_COL], mv[:, q, 0]).then_inc(s.cols_done, 1)

            def scatter(g, s):
                pool.wait_ge(s.rows_done, g + 1)
                pool.wait_ge(s.xn_done, g + 1)
                if g == 0 and n == 0:
                    pool.wait_ge(s.xn_done0, 1)
                pool.wait_ge(s.slots_set, 1)
                pool.wait_ge(s.rows_set, 16)
                pool.wait_ge(s.cols_done, 2 * g + 2)
                if s is layers[0] and g == 0:
                    pool.wait_ge(zero_out, 64)
                for t in range(g * GROUP, (g + 1) * GROUP):
                    pool.indirect_dma_start(disp[:, :], bass.IndirectOffsetOnAxis(ap=to_row[:, t:t + 1], axis=0),
                                            xn[:, t, :], None).then_inc(s.scattered, 16)

            def set_rows(s):
                pool.dma_start(disp[0:SLOTS, TOKEN_COL].rearrange("(p r) -> p r", p=P),
                               slot_rows[:, :], allow_slow_non_contiguous=True).then_inc(s.rows_set, 16)

            s0 = layers[0]
            for n, s in enumerate(layers):
                pool.sem_inc(s.eotok_free, 1)
                pool.iota(xn[:, :, TOKEN_COL], [[P, TILES]], base=0, channel_multiplier=1,
                          allow_small_or_imprecise_dtypes=True).then_inc(s.slots_set, 1)
                if n == 0:
                    pool.wait_ge(pool_const, 10)
                else:
                    pool.wait_ge(s0.dtok_in, 32 * (E + 1))
                set_rows(s)
                if n == 0:
                    for g in range(GROUPS):
                        power(g, s.var_done, s.rstd_done)
                        columns(g, s)
                    for g in range(GROUPS):
                        scatter(g, s)
                else:
                    pool.wait_ge(n_var, 1)
                    for c in (0, SEQ + 1):
                        pool.memset(xT[:, :, c:c + 1], 0.0).then_inc(n_pad, 1)
                    power(0, n_var, n_rstd)
                    for g in range(GROUPS + 2):
                        if g + 1 < GROUPS:
                            power(g + 1, n_var, n_rstd)
                        if g >= 2:
                            power(g - 2, s.var_done, s.rstd_done)
                            columns(g - 2, s)
                    for g in range(GROUPS):
                        scatter(g, s)

                target = (x1, out)[n]

                def expert(e, s=s, target=target):
                    pool.wait_ge(s.meta, 4 * e + 4)
                    pool.wait_ge(s.kept, 16 * (UNITS if s is s0 else GROUPS))
                    for i, (k, _) in enumerate(HELD):
                        m = PARTS[k][1]
                        pool.wait_ge(s.out_dve, 3 + 3 * e + i + 1)
                        pool.sem_inc(s.may_send, 1)
                        pool.indirect_dma_start(target[:, :],
                                                bass.IndirectOffsetOnAxis(ap=res_row[0:m, k:k + 1], axis=0),
                                                eotok[0:m, k, :], None).then_inc(s.res_out, 16)
                    pool.wait_ge(s.res_out, 48 * e + 48)
                    pool.sem_inc(s.eotok_free, 1)

                with pool.Fori(0, E) as e:
                    expert(e)

        @block.scalar
        def _(act):
            copy = ACT.Copy
            for n, s in enumerate(layers):
                act.sem_inc(s.gelu_done, ICS)
                act.sem_inc(s.eoT_done, 1)

                def norm(g, rstd_sem, xn_sem, tiles=GROUP):
                    act.wait_ge(rstd_sem, 2 * (g + 1))
                    for t in range(g * GROUP, g * GROUP + tiles):
                        ins = act.activation(xn[:, t, 0:D], xt[:, t, :], ACT.Identity,
                                             bias=shift[:, t:t + 1], scale=rstd[:, t:t + 1])
                    ins.then_inc(xn_sem, 1)

                def copy_tokens(g, s=s):
                    for c in range(DC):
                        act.wait_ge(s.xT_done, DC * g + c + 1)
                        if c == 0 and g >= 2:
                            act.wait_ge(s.logits_done, g - 1)
                        act.activation(xTt[:, g % 2, c, :], psT[c % 2][:, :], copy).then_inc(s.xT_copied, 1)

                def exps(g, s=s):
                    act.wait_ge(s.diff_done, g + 1)
                    act.activation(sel[:, g % 2], sel[:, g % 2], ACT.Exp).then_inc(s.exp_done, 1)

                if n == 0:
                    norm(0, s.rstd_done, s.xn_done, GROUP // 2)
                for g in range(GROUPS):
                    if n == 1 and g >= 2:
                        norm(g, s.rstd_done, s.xn_done)
                    if n == 0 or g >= 2:
                        copy_tokens(g)
                    if n == 0 and g + 1 < GROUPS:
                        norm(g + 1, s.rstd_done, s.xn_done)
                    if g >= 2:
                        exps(g - 2)
                exps(GROUPS - 2)
                exps(GROUPS - 1)
                act.preload_act_table(ACT.Gelu)

                def wi_split(e, step, s=s):
                    k = (step // 2) % 2
                    if step % 2 == 0:
                        act.wait_ge(s.wi_in[k], 32 * e + 16 * (step // 4 + 1))
                    act.wait_ge(s.h_ready, ICS * STEPS * e + ICS * (step + 1))
                    act.activation(wih[:, step % 2, :, :],
                                   raw_wi[k][:, :, (step % 2) * HALF:(step % 2 + 1) * HALF],
                                   copy).then_inc(s.wi_hi, 1)

                def wo_split(e, step, s=s):
                    k = (step // 2) % 2
                    if step % 2 == 0:
                        act.wait_ge(s.wo_in[k], 32 * e + 16 * (step // 4 + 1))
                    act.wait_ge(s.mm2_done, STEPS * e + step + 1)
                    act.activation(woh[:, step % 2, :, :],
                                   raw_wo[k][:, (step % 2) * ICS:(step % 2 + 1) * ICS, :],
                                   copy).then_inc(s.wo_hi, 1)

                def tokens(e, c, s=s, bank=None):
                    act.wait_ge(s.tokT_done, DC * e + c + 1)
                    act.activation(dth[:, c, :], (bank or psT[c % 2])[:, 0:CAP], copy).then_inc(s.dt_hi, 1)

                wi_split(0, 0)
                wi_split(0, 1)
                for c in range(DC):
                    tokens(0, c, bank=FIRST[c])
                wo_split(0, 0)

                def expert(e, last, s=s):
                    for step in range(STEPS):
                        act.wait_ge(s.ht_lo, STEPS * e + step + 1)
                        for j in range(ICS):
                            ic = ICS * step + j
                            act.wait_ge(s.h_ready, 2 * ICS + ICS * STEPS * e + ic + 1)
                            act.activation(gel[:, step % 2, j, :], psH[j][:, 0:CAP],
                                           ACT.Gelu).then_inc(s.gelu_done, 1)
                        if step == STEPS - 1:
                            tokens(e + 1, 0)
                            tokens(e + 1, 1)
                        if not last or step + 2 < STEPS:
                            wi_split(e, step + 2)
                        if step == STEPS - 1:
                            tokens(e + 1, 2)
                            tokens(e + 1, 3)
                        if not last or step + 1 < STEPS:
                            wo_split(e, step + 1)
                        if 1 <= step <= len(PARTS):
                            k = step - 1
                            m = PARTS[k][1]
                            act.wait_ge(s.out_dve, 3 + 3 * e)
                            act.wait_ge(s.dtok_in, 32 * e + 32)
                            act.activation(xr[0:m, k, :], dtok[0:m, k, 0:D], ACT.Identity,
                                           bias=dtok[0:m, k, MEAN_COL:MEAN_COL + 1],
                                           scale=dtok[0:m, k, STD_COL:STD_COL + 1]).then_inc(s.xr_done, 1)
                        if last and s is layers[0]:
                            k, c = divmod(step, DC)
                            if step == 0:
                                act.wait_ge(w_raw_in, 64)
                                act.activation(wg1[0][:, :, :], raw_g1[:, :, :], copy).then_inc(g_hi, 1)
                                act.activation(wg2[0][:, :], raw_g2[:, :], copy).then_inc(g_hi, 1)
                            act.activation((wu, wv)[k][0][:, c, :], raw_u[k][:, c, :], copy).then_inc(uv_hi, 1)
                    for c in range(DC):
                        act.wait_ge(s.acc_done, DC * e + c + 1)
                        act.activation(eoT[:, c, :], acc[c][:, 0:CAP], copy).then_inc(s.eoT_done, 1)

                with act.Fori(0, E - 1) as e:
                    expert(e, False)
                expert(E - 1, True)

                if n == 1:
                    break
                nxt = layers[1]
                def place(g):
                    return 1 + (g % 2) * GT

                def take_xT(g):
                    if g == 2:
                        act.wait_ge(d_tap, 2 * DC)
                    if g == 3:
                        act.wait_ge(d_conv, 2 * DC)
                    if g >= 2:
                        act.wait_ge(p_ring, i_v(g - 2, DC - 1) + 1)
                    for c in range(DC):
                        act.wait_ge(n_T, DC * g + c + 1)
                        act.activation(xT[:, c, place(g):place(g) + GT], psT[c % 2][:, :], copy).then_inc(n_xT, 1)
                        act.wait_ge(n_xT, DC * g + c + 1)
                        act.activation(xTh[g % 2][:, c, :], xT[:, c, place(g):place(g) + GT],
                                       copy).then_inc(n_xTh, 1)

                def conv_mid(g):
                    for c in range(DC):
                        act.activation(convT(g, c), xT[:, c, place(g):place(g) + GT], ACT.Identity,
                                       bias=small[:, CB0 + c:CB0 + c + 1],
                                       scale=small[:, CW0 + 3 * c + 1:CW0 + 3 * c + 2]).then_inc(a_conv, 1)

                def relu(g):
                    act.wait_ge(p_ring, i_h(g) + 1)
                    if g >= 1:
                        act.wait_ge(d_hl, g)
                    act.activation(hid[:, :], acc[i_h(g) % 4][:, :], ACT.Relu,
                                   bias=small[:, BG10:BG10 + 1]).then_inc(a_h, 1)

                def glob_hi(i):
                    g, c = divmod(i, DC)
                    act.wait_ge(d_glob, i + 1)
                    if g >= 2:
                        act.wait_ge(p_uv, GROUP * (g - 1))
                    act.activation(glh[:, g % 2, c, :], vg[c % 2][:, :], copy).then_inc(a_glh, 1)

                norm(0, n_rstd, n_xn, GROUP // 2)
                take_xT(0)
                relu(0)
                for g in range(GROUPS):
                    more = g + 1 < GROUPS
                    for c in range(DC):
                        i = DC * g + c
                        act.wait_ge(p_ring, i_gate(g, c) + 1)
                        if i >= 1:
                            act.wait_ge(d_vg, i)
                        act.activation(gate[:, :], acc[i_gate(g, c) % 4][:, :], ACT.Sigmoid,
                                       bias=small[:, BG20 + c:BG20 + c + 1]).then_inc(a_gate, 1)
                        if i >= 1:
                            glob_hi(i - 1)
                        if c == 0:
                            conv_mid(g)
                        if c == 1:
                            if more:
                                norm(g + 1, n_rstd, n_xn)
                        if c == 2:
                            if more:
                                take_xT(g + 1)
                            else:
                                copy_tokens(0, nxt)
                        if c == 3:
                            if more:
                                relu(g + 1)
                            if g >= 2:
                                norm(g - 2, nxt.rstd_done, nxt.xn_done)
                glob_hi(DC * GROUPS - 1)
                copy_tokens(1, nxt)
                act.preload_act_table(ACT.Exp)

        @block.vector
        def _(dve):
            seq = [0]

            def then(ins):
                ins.then_inc(dve_seq, 1)
                seq[0] += 1

            def settle():
                dve.wait_ge(dve_seq, seq[0])

            def lo(out, full, hi):
                return dve.tensor_tensor(out, full, hi.bitcast(F32), ALU.subtract)

            def moments(g, var_sem, loaded):
                q = slice(g * GROUP, (g + 1) * GROUP)
                for j in range(GROUP):
                    if loaded and (j == 0 or loaded[j] is not loaded[j - 1]):
                        dve.wait_ge(loaded[j], 16)
                    then(dve.bn_stats(stats[:, j, :], xt[:, g * GROUP + j, :]))
                settle()
                for j in range(GROUP):
                    then(dve.bn_aggr(mv[:, g * GROUP + j, :], stats[:, j, :]))
                settle()
                then(dve.tensor_scalar(neg_mean[:, q], mv[:, q, 0], -1.0, None, ALU.mult))
                settle()
                dve.tensor_scalar(var[:, q], mv[:, q, 1], EPS, None, ALU.add).then_inc(var_sem, 1)

            def norm_half(rstd_sem, xn0_sem):
                dve.wait_ge(rstd_sem, 1)
                for t in range(GROUP // 2, GROUP):
                    ins = dve.tensor_scalar(xn[:, t, 0:D], xt[:, t, :], mv[:, t, 0:1], rstd[:, t:t + 1],
                                            ALU.subtract, ALU.mult)
                ins.then_inc(xn0_sem, 1)

            by_t = "p e t -> p t e"

            def over(a, k):
                return t4[:, a, k:k + 1, :].to_broadcast(each)

            def route(g, s):
                new, old = g < GROUPS, g >= 1
                a, b = g % 2, (g - 1) % 2
                q = slice((g - 1) * GROUP, g * GROUP)
                if new:
                    dve.wait_ge(s.logits_done, g + 1)
                    dve.tensor_copy(lgT[:, :], ps_logitT[a]).then_inc(s.lgT_copied, 1)
                    dve.wait_ge(s.lg_turned, g + 1)
                    dve.tensor_copy(lg[:, :, :], ps_logit[a].rearrange("p (t e) -> p e t", e=E)
                                    ).then_inc(s.lg_copied, 1)
                if old:
                    dve.wait_ge(s.rank_done, g)
                    dve.tensor_tensor(r8[:, b], ps_rank[b].rearrange("p (e t) -> p e t", e=E), ohb[:, b],
                                      ALU.mult).then_inc(s.rank_used, 1)
                    dve.wait_ge(s.exp_done, g)
                    then(dve.tensor_reduce(t4[:, b, 2, :], sel[:, b].rearrange(by_t), AX_X, ALU.add))
                if new:
                    dve.wait_ge(s.lg_copied, g + 1)
                    then(dve.tensor_reduce(t4[:, a, 0, :], lg[:, :, :].rearrange(by_t), AX_X, ALU.max))
                if old:
                    dve.wait_ge(s.rank_used, g)
                    then(dve.tensor_reduce(t4[:, b, 4, :], r8[:, b].rearrange(by_t), AX_X, ALU.add))
                settle()
                if new:
                    dve.tensor_tensor(sel[:, a], lg[:, :, :], over(a, 0), ALU.subtract).then_inc(s.diff_done, 1)
                    then(dve.tensor_tensor(r8[:, a], lg[:, :, :], over(a, 0), ALU.is_equal))
                if old:
                    then(dve.reciprocal(t4[:, b, 3, :], t4[:, b, 2, :]))
                    then(dve.tensor_scalar(t4[:, b, 6, :], t4[:, b, 4, :], float(CAP), None, ALU.is_le))
                    then(dve.tensor_tensor(t4[:, b, 7, :], t4[:, b, 4, :], t4[:, b, 5, :], ALU.add))
                settle()
                if new:
                    then(dve.tensor_tensor(r8[:, a], r8[:, a], desc[:, :, :], ALU.mult))
                if old:
                    then(dve.tensor_tensor(t4[:, b, 8, :], t4[:, b, 7, :], spare[:, q], ALU.subtract))
                    then(dve.scalar_tensor_tensor(xn[:, q, W_COL], t4[:, b, 3, :], 0.5, t4[:, b, 6, :],
                                                  ALU.mult, ALU.mult))
                settle()
                if new:
                    then(dve.tensor_reduce(t4[:, a, 1, :], r8[:, a].rearrange(by_t), AX_X, ALU.max))
                if old:
                    then(dve.tensor_tensor(t4[:, b, 8, :], t4[:, b, 8, :], t4[:, b, 6, :], ALU.mult))
                settle()
                if new:
                    dve.tensor_tensor(ohb[:, a], desc[:, :, :], over(a, 1), ALU.is_equal).then_inc(s.oh_done, 1)
                if old:
                    dve.tensor_tensor(to_row[:, q], t4[:, b, 8, :], spare[:, q], ALU.add).then_inc(s.rows_done, 1)
                if new:
                    dve.wait_ge(s.oh_done, g + 1)
                    then(dve.tensor_reduce(lg[:, :, 0], ohb[:, a], AX_X, ALU.add))
                    then(dve.tensor_tensor(r8[:, a], slot0[:, :, :], ohb[:, a], ALU.mult))
                    settle()
                    then(dve.tensor_tensor(so_far[:, :], so_far[:, :], lg[:, :, 0], ALU.add))
                    then(dve.tensor_reduce(t4[:, a, 5, :], r8[:, a].rearrange(by_t), AX_X, ALU.add))
                    settle()
                    dve.tensor_copy(before[:, g + 1, :], so_far[:, :]).then_inc(s.before_done, 1)

            def all_taken(s):
                dve.wait_ge(s.rank_done, GROUPS + 1)
                dve.tensor_copy(taken[:, 0:E], ps_logit[0][:, 0:E]).then_inc(s.taken_done, 1)

            def start_count(s):
                then(dve.memset(so_far[:, :], 0.0))
                dve.memset(before[:, 0, :], 0.0).then_inc(s.before_done, 1)

            dve.memset(zeros[:, :], 0.0).then_inc(dve_const, 1)
            then(dve.memset(taken[:, E:E + 1], 0))
            then(dve.memset(one_col[:, :], 1.0))

            for n, s in enumerate(layers):
                dve.sem_inc(s.ht_lo, 2)
                dve.sem_inc(s.out_dve, 3)
                if n == 0:
                    start_count(s)
                    moments(0, s.var_done, x_tile)
                    norm_half(s.rstd_done, s.xn_done0)
                    for g in range(1, GROUPS):
                        moments(g, s.var_done, [x_in[g - 1]] * GROUP)
                    dve.wait_ge(pool_const, 10)
                for g in range(n, GROUPS + 1):
                    route(g, s)
                all_taken(s)
                if n == 0:
                    dve.wait_ge(s.taken_done, 1)
                    for bank in (*acc, *psH):
                        then(dve.memset(bank[:, :], 0.0))

                def wi_split(e, step, s=s):
                    k = (step // 2) % 2
                    dve.wait_ge(s.wi_hi, STEPS * e + step + 1)
                    lo(wil[:, step % 2, :, :], raw_wi[k][:, :, (step % 2) * HALF:(step % 2 + 1) * HALF],
                       wih[:, step % 2, :, :]).then_inc(s.wi_lo, 1)

                def wo_split(e, step, s=s):
                    k = (step // 2) % 2
                    dve.wait_ge(s.wo_hi, STEPS * e + step + 1)
                    lo(wol[:, step % 2, :, :], raw_wo[k][:, (step % 2) * ICS:(step % 2 + 1) * ICS, :],
                       woh[:, step % 2, :, :]).then_inc(s.wo_lo, 1)

                def tokens(e, c, s=s, bank=None):
                    dve.wait_ge(s.dt_hi, DC * e + c + 1)
                    lo(dtl[:, c, :], (bank or psT[c % 2])[:, 0:CAP], dth[:, c, :]).then_inc(s.dt_lo, 1)

                wi_split(0, 0)
                wi_split(0, 1)
                for c in range(DC):
                    tokens(0, c, bank=FIRST[c])
                wo_split(0, 0)

                def expert(e, last, s=s):
                    for step in range(STEPS):
                        k = step % 2
                        dve.wait_ge(s.gelu_done, ICS + ICS * (STEPS * e + step + 1))
                        dve.wait_ge(s.mm2_done, STEPS * e + step + 1)
                        dve.tensor_copy(hth[:, k, :, :], gel[:, k, :, :]).then_inc(s.ht_hi, 1)
                        dve.wait_ge(s.ht_hi, STEPS * e + step + 1)
                        lo(htl[:, k, :, :], gel[:, k, :, :], hth[:, k, :, :]).then_inc(s.ht_lo, 1)
                        if step == STEPS - 1:
                            tokens(e + 1, 0)
                            tokens(e + 1, 1)
                        if not last or step + 2 < STEPS:
                            wi_split(e, step + 2)
                        if step == STEPS - 1:
                            tokens(e + 1, 2)
                            tokens(e + 1, 3)
                        if not last or step + 1 < STEPS:
                            wo_split(e, step + 1)
                        if step == 2:
                            dve.wait_ge(s.dtok_in, 32 * e + 32)
                            dve.wait_ge(s.eotok_free, e + 1)
                            for m, parts in ((P, slice(0, 2)), (PARTS[2][1], slice(2, 3))):
                                dve.tensor_copy(slot_w[0:m, parts], dtok[0:m, parts, W_COL]).then_inc(s.meta, 1)
                                dve.tensor_copy(res_row[0:m, parts], dtok[0:m, parts, TOKEN_COL]
                                                ).then_inc(s.meta, 1)
                        if last and s is layers[0]:
                            k, c = divmod(step, DC)
                            if step == 0:
                                dve.wait_ge(g_hi, 2)
                                lo(wg1[1][:, :, :], raw_g1[:, :, :], wg1[0][:, :, :]).then_inc(g_lo, 1)
                                lo(wg2[1][:, :], raw_g2[:, :], wg2[0][:, :]).then_inc(g_lo, 1)
                            dve.wait_ge(uv_hi, step + 1)
                            w = (wu, wv)[k]
                            lo(w[1][:, c, :], raw_u[k][:, c, :], w[0][:, c, :]).then_inc(uv_lo, 1)
                    dve.wait_ge(s.eotok_free, e + 1)
                    dve.wait_ge(s.meta, 4 * e + 4)
                    dve.wait_ge(s.xr_done, 3 * e + 3)
                    for i, (k, bank) in enumerate(HELD):
                        m = PARTS[k][1]
                        dve.wait_ge(s.outT_done, 3 * e + i + 1)
                        dve.scalar_tensor_tensor(eotok[0:m, k, :], bank[0:m, :], slot_w[0:m, k:k + 1],
                                                 xr[0:m, k, :], ALU.mult, ALU.add).then_inc(s.out_dve, 1)

                with dve.Fori(0, E - 1) as e:
                    expert(e, False)
                expert(E - 1, True)

                if n == 1:
                    break
                nxt = layers[1]

                def place(g):
                    return 1 + (g % 2) * GT

                def xT_lo(g):
                    for c in range(DC):
                        dve.wait_ge(n_xTh, DC * g + c + 1)
                        if c == 0 and g >= 2:
                            dve.wait_ge(p_ring, i_v(g - 2, DC - 1) + 1)
                        lo(xTl[g % 2][:, c, :], xT[:, c, place(g):place(g) + GT],
                           xTh[g % 2][:, c, :]).then_inc(n_xTl, 1)

                def split_h(g):
                    dve.wait_ge(a_h, g + 1)
                    dve.tensor_copy(hh[:, :], hid[:, :]).then_inc(d_hh, 1)
                    dve.wait_ge(d_hh, g + 1)
                    lo(hl[:, :], hid[:, :], hh[:, :]).then_inc(d_hl, 1)

                def glob_lo(i):
                    g, c = divmod(i, DC)
                    dve.wait_ge(a_glh, i + 1)
                    lo(gll[:, g % 2, c, :], vg[c % 2][:, :], glh[:, g % 2, c, :]).then_inc(d_gll, 1)

                def adds(w):
                    dve.wait_ge(p_conv, w + 1)
                    dve.tensor_tensor(xt[:, w, :], psT[w % 2][:, :], xt[:, w, :], ALU.add).then_inc(d_addc, 1)
                    dve.wait_ge(p_uv, w + 1)
                    dve.wait_ge(d_addc, w + 1)
                    dve.tensor_tensor(xt[:, w, :], psH[w % 2][:, :], xt[:, w, :], ALU.add).then_inc(d_addu, 1)

                def chain(g, c):
                    i = DC * g + c
                    dve.wait_ge(a_gate, i + 1)
                    dve.wait_ge(p_ring, i_u(g, c) + 1)
                    if i >= 1:
                        dve.wait_ge(d_glob, i)
                    dve.scalar_tensor_tensor(ug[:, :], acc[i_u(g, c) % 4][:, :], small[:, BU0 + c:BU0 + c + 1],
                                             gate[:, :], ALU.add, ALU.mult).then_inc(d_ug, 1)
                    if i >= 1:
                        glob_lo(i - 1)
                    dve.wait_ge(d_ug, i + 1)
                    start = 0.0 if g % 2 == 0 else carry[:, c:c + 1]
                    then(dve.tensor_tensor_scan(ug[:, :], one_col[:, :].to_broadcast([P, GT]), ug[:, :],
                                                start, ALU.mult, ALU.add))
                    if GROUP * (g - 1) + c >= 1:
                        adds(GROUP * (g - 1) + c - 1)
                    if c == DC - 1 and g + 1 < GROUPS:
                        split_h(g + 1)
                    dve.wait_ge(p_ring, i_v(g, c) + 1)
                    dve.scalar_tensor_tensor(vg[c % 2][:, :], acc[i_v(g, c) % 4][:, :],
                                             small[:, BV0 + c:BV0 + c + 1],
                                             gate[:, :], ALU.add, ALU.mult).then_inc(d_vg, 1)
                    settle()
                    dve.wait_ge(d_vg, i + 1)
                    if g % 2 == 0:
                        then(dve.tensor_copy(carry[:, c:c + 1], ug[:, GT - 1:GT]))
                    dve.tensor_tensor(vg[c % 2][:, :], vg[c % 2][:, :], ug[:, :], ALU.mult).then_inc(d_glob, 1)

                def tap(g, k):
                    q = place(g) + k - 1
                    if k == 0:
                        dve.wait_ge(n_pad, 2)
                    else:
                        dve.wait_ge(n_xT, DC * (g + 2 - g % 2))
                    for c in range(DC):
                        dve.wait_ge(d_tap if k else a_conv, DC * g + c + 1)
                        dve.scalar_tensor_tensor(
                            convT(g, c), xT[:, c, q:q + GT],
                            small[:, CW0 + 3 * c + k:CW0 + 3 * c + k + 1], convT(g, c),
                            ALU.mult, ALU.add).then_inc(d_conv if k else d_tap, 1)

                def next_moments(g):
                    dve.wait_ge(d_addu, GROUP * (g + 1))
                    moments(g, nxt.var_done, None)

                moments(0, n_var, x1_tile)
                norm_half(n_rstd, n_xn0)
                xT_lo(0)
                split_h(0)
                for g in range(GROUPS):
                    more = g + 1 < GROUPS
                    for c in range(DC):
                        chain(g, c)
                        if c == 0 and more:
                            moments(g + 1, n_var, [x1_in[g]] * GROUP)
                        if c == 1:
                            tap(g, 0)
                        if c == 2:
                            if more:
                                xT_lo(g + 1)
                            if g >= 2:
                                next_moments(g - 2)
                        if c == 3:
                            tap(g, 2)
                glob_lo(DC * GROUPS - 1)
                adds(GROUP * (GROUPS - 1) - 1)
                next_moments(GROUPS - 2)
                start_count(nxt)
                for j in range(GROUP):
                    adds(GROUP * (GROUPS - 1) + j)
                next_moments(GROUPS - 1)
                route(0, nxt)

        @block.tensor
        def _(pe):
            def product(out, lhs, rhs, first, last):
                (lh, ll), (rh, rl) = lhs, rhs
                pe.matmul(out, lh, rh, start=first, stop=False)
                pe.matmul(out, lh, rl, start=False, stop=False)
                return pe.matmul(out, ll, rh, start=False, stop=last)

            turned = []

            def turn_bank(freed_by, value):
                k = len(turned)
                if k >= 2:
                    pe.wait_ge(*turned[k - 2])
                turned.append((freed_by, value))
                return psT[k % 2]

            tokens = pe.alloc_register("tokens")
            pe.wait_ge(pool_const, 10)
            for n, s in enumerate(layers):
                pe.sem_inc(s.h_ready, 2 * ICS)
                pe.sem_inc(s.mm2_done, 2)

                def turn(g, s=s):
                    pe.wait_ge(s.xn_done, g + 1)
                    if g == 0 and s is layers[0]:
                        pe.wait_ge(s.xn_done0, 1)
                    for c in range(DC):
                        to = turn_bank(s.xT_copied, DC * g + c + 1)
                        for j in range(GROUP):
                            ins = pe.transpose(to[:, j * P:(j + 1) * P],
                                               xn[:, GROUP * g + j, c * P:(c + 1) * P], ident[:, :])
                        ins.then_inc(s.xT_done, 1)

                def logits(g, s=s):
                    pe.wait_ge(s.xT_copied, DC * g + DC)
                    if g == 0:
                        if s is layers[0]:
                            pe.wait_ge(small_loaded, 16)
                        else:
                            pe.wait_ge(d_vg, DC * GROUPS)
                    if g >= 2:
                        pe.wait_ge(s.lg_copied, g - 1)
                    for c in range(DC):
                        ins = pe.matmul(ps_logitT[g % 2], small[:, GATE0 + c * E:GATE0 + (c + 1) * E],
                                        xTt[:, g % 2, c, :], start=(c == 0), stop=(c == DC - 1))
                    ins.then_inc(s.logits_done, 1)

                def logits_by_tokens(g, s=s):
                    pe.wait_ge(s.lgT_copied, g + 1)
                    for j in range(GROUP):
                        ins = pe.transpose(ps_logit[g % 2][:, j * E:(j + 1) * E], lgT[:, j * P:(j + 1) * P],
                                           ident[0:E, 0:E])
                    ins.then_inc(s.lg_turned, 1)

                def ranks(g, s=s):
                    a = g % 2
                    out = ps_rank[a].rearrange("p (e t) -> p e t", e=E)
                    pe.wait_ge(s.oh_done, g + 1)
                    pe.wait_ge(s.before_done, g + 1)
                    if g >= 2:
                        pe.wait_ge(s.rank_used, g - 1)
                    pe.matmul(out, tri[:, :], ohb[:, a], start=True, stop=False)
                    for k in range(1, GROUP):
                        pe.matmul(out[:, :, k:], ones[:, :], ohb[:, a, :, 0:GROUP - k], start=False, stop=False)
                    pe.matmul(out, ones[:, :], before[:, g, :].unsqueeze(2).to_broadcast(each),
                              start=False, stop=True).then_inc(s.rank_done, 1)

                if n == 0:
                    turn(0)
                for g in range(GROUPS):
                    if n == 0 or g >= 1:
                        logits(g)
                        if g + 1 < GROUPS:
                            turn(g + 1)
                        logits_by_tokens(g)
                    if g >= 1:
                        ranks(g - 1)
                ranks(GROUPS - 1)
                pe.wait_ge(s.before_done, GROUPS + 1)
                pe.wait_ge(s.lg_copied, GROUPS)
                pe.matmul(ps_logit[0][:, 0:E], ones[:, :], before[:, GROUPS, :],
                          start=True, stop=True).then_inc(s.rank_done, 1)

                def turn_tokens(e, c, s=s, bank=None):
                    pe.wait_ge(s.dtok_in, 32 * e + 32)
                    if c >= 2 and not bank:
                        pe.wait_ge(s.dt_lo, DC * e + c - 1)
                    for k, (q, m) in enumerate(PARTS):
                        ins = pe.transpose((bank or psT[c % 2])[:, q:q + m], dtok[0:m, k, c * P:(c + 1) * P], ident[0:m, 0:m])
                    ins.then_inc(s.tokT_done, 1)

                def mm1(e, step, w, s=s):
                    k = step % 2
                    pe.wait_ge(s.wi_lo, STEPS * e + step + 1)
                    for j in range(ICS):
                        ic = ICS * step + j
                        if step > 0:
                            pe.wait_ge(s.gelu_done, ICS * STEPS * e + ic + 1)
                        if ic == 1:
                            pe.wait_ge(s.out_dve, 3 * e + 2)
                        for c in range(DC):
                            i = slice(j * P, (j + 1) * P)
                            ins = product(psH[j][:, 0:w], (wih[:, k, c, i], wil[:, k, c, i]),
                                          (dth[:, c, 0:w], dtl[:, c, 0:w]), c == 0, c == DC - 1)
                        ins.then_inc(s.h_ready, 1)

                def mm2(e, step, w, s=s):
                    k = step % 2
                    pe.wait_ge(s.wo_lo, STEPS * e + step + 1)
                    pe.wait_ge(s.ht_lo, 2 + STEPS * e + step + 1)
                    for c in range(DC):
                        for j in range(ICS):
                            d = slice(c * P, (c + 1) * P)
                            ins = product(acc[c][:, 0:w], (woh[:, k, j, d], wol[:, k, j, d]),
                                          (hth[:, k, j, 0:w], htl[:, k, j, 0:w]),
                                          step == 0 and j == 0, step == STEPS - 1 and j == ICS - 1)
                        if step == STEPS - 1 and c < DC - 1:
                            ins.then_inc(s.acc_done, 1)
                    return ins

                def turn_out(e, s=s):
                    pe.wait_ge(s.dt_lo, DC * (e + 1) + DC)
                    for c in range(DC):
                        pe.wait_ge(s.eoT_done, 1 + DC * e + c + 1)
                        for i, (k, bank) in enumerate(HELD):
                            q, m = PARTS[k]
                            ins = pe.transpose(bank[0:m, c * P:(c + 1) * P], eoT[:, c, q:q + m], ident[:, :])
                            if c == 0 and i == 0:
                                ins.then_inc(s.mm2_done, 1)
                            if c == DC - 1:
                                ins.then_inc(s.outT_done, 1)

                pe.wait_ge(s.wi_lo, 1)
                for c in range(DC):
                    turn_tokens(0, c, bank=FIRST[c])

                def expert(e, w):
                    mm1(e, 0, w)
                    for step in range(1, STEPS):
                        mm1(e, step, w)
                        if step == STEPS - 1:
                            turn_tokens(e + 1, 0)
                            turn_tokens(e + 1, 1)
                        mm2(e, step - 1, w).then_inc(s.mm2_done, 1)
                    turn_tokens(e + 1, 2)
                    turn_tokens(e + 1, 3)
                    pe.reg_load(tokens, taken[0:1, bass.ds(e + 1, 1)])
                    mm2(e, STEPS - 1, w).then_inc(s.acc_done, 1)
                    turn_out(e)

                def at_width(e, widths):
                    if len(widths) == 1:
                        expert(e, widths[0])
                        return
                    half = len(widths) // 2
                    with pe.If_lt(tokens, widths[half - 1] + 1):
                        at_width(e, widths[:half])
                    with pe.Else():
                        at_width(e, widths[half:])

                pe.wait_ge(s.taken_done, 1)
                pe.wait_ge(s.dt_lo, DC)
                pe.reg_load(tokens, taken[0:1, 0:1])
                with pe.Fori(0, E) as e:
                    at_width(e, WIDTHS)

                if n == 1:
                    break
                used = []

                def bank(freed_by, value):
                    u = len(used)
                    if u >= 4:
                        pe.wait_ge(*used[u - 4])
                    used.append((freed_by, value))
                    return acc[u % 4][:, :]

                turned.clear()

                def turn_group(g):
                    pe.wait_ge(n_xn, g + 1)
                    if g == 0:
                        pe.wait_ge(n_xn0, 1)
                    for c in range(DC):
                        to = turn_bank(n_xT, DC * g + c + 1)
                        for j in range(GROUP):
                            ins = pe.transpose(to[:, j * P:(j + 1) * P],
                                               xn[:, GROUP * g + j, c * P:(c + 1) * P], ident[:, :])
                        ins.then_inc(n_T, 1)

                def turn_conv(g, j):
                    if j == 0:
                        pe.wait_ge(d_conv, DC * (g + 1))
                    to = turn_bank(d_addc, GROUP * g + j + 1)
                    for c in range(DC):
                        ins = pe.transpose(to[:, c * P:(c + 1) * P], convT(g, c)[:, j * P:(j + 1) * P],
                                           ident[:, :])
                    ins.then_inc(p_conv, 1)

                def times_wu(g, j):
                    w = GROUP * g + j
                    a = g % 2
                    if j == 0:
                        pe.wait_ge(d_gll, DC * (g + 1))
                    if w >= 2:
                        pe.wait_ge(d_addu, w - 1)
                    q = slice(j * P, (j + 1) * P)
                    for c in range(DC):
                        ins = product(psH[j % 2][:, :], (glh[:, a, c, q], gll[:, a, c, q]),
                                      (wu[0][:, c, :], wu[1][:, c, :]), c == 0, c == DC - 1)
                    ins.then_inc(p_uv, 1)

                def hidden(g):
                    a = g % 2
                    to = bank(a_h, g + 1)
                    for c in range(DC):
                        pe.wait_ge(n_xTl, DC * g + c + 1)
                        ins = product(to, (wg1[0][:, c, :], wg1[1][:, c, :]), (xTh[a][:, c, :], xTl[a][:, c, :]),
                                      c == 0, c == DC - 1)
                    ins.then_inc(p_ring, 1)

                def projection(g, w, c, freed_by):
                    a = g % 2
                    to = bank(freed_by, DC * g + c + 1)
                    r = slice(c * P, (c + 1) * P)
                    for k in range(DC):
                        ins = product(to, (w[0][:, k, r], w[1][:, k, r]), (xTh[a][:, k, :], xTl[a][:, k, :]),
                                      k == 0, k == DC - 1)
                    ins.then_inc(p_ring, 1)

                nxt = layers[1]
                turn_group(0)
                pe.wait_ge(g_lo, 2)
                pe.wait_ge(uv_lo, 2 * DC)
                hidden(0)
                for g in range(GROUPS):
                    more = g + 1 < GROUPS
                    for c in range(DC):
                        if c == 0:
                            pe.wait_ge(d_hl, g + 1)
                        to = bank(a_gate, DC * g + c + 1)
                        r = slice(c * P, (c + 1) * P)
                        product(to, (wg2[0][:, r], wg2[1][:, r]), (hh[:, :], hl[:, :]), True, True).then_inc(p_ring, 1)
                        projection(g, wu, c, d_ug)
                        if c == DC - 1 and more:
                            hidden(g + 1)
                        projection(g, wv, c, d_vg)
                        if c == 2:
                            if more:
                                turn_group(g + 1)
                            else:
                                turn(0, nxt)
                        if g >= 1:
                            turn_conv(g - 1, c)
                            times_wu(g - 1, c)
                for j in range(GROUP):
                    turn_conv(GROUPS - 1, j)
                    times_wu(GROUPS - 1, j)
                    if j == 1:
                        turn(1, nxt)
                logits(0, nxt)
                logits_by_tokens(0, nxt)

def kernel(L0_attn_x, L0_attn_Wu, L0_attn_bu, L0_attn_Wv, L0_attn_bv, L0_attn_Wg1, L0_attn_bg1, L0_attn_Wg2,
           L0_attn_bg2, L0_attn_conv_w, L0_attn_conv_b, L0_ffn_gate_weight, L0_ffn_wi, L0_ffn_wo):
    import numpy as np
    import concourse.bacc as bacc
    from concourse.bass_utils import run_bass_kernel_spmd

    def cols(v):
        v = np.asarray(v).reshape(np.shape(v)[0] // P, P, -1)
        return v.transpose(1, 0, 2).reshape(P, -1)

    small = np.zeros((P, SMALL), np.float32)
    small[:, GATE0:BU0] = cols(np.asarray(L0_ffn_gate_weight).T)
    small[:, BU0:BV0] = cols(L0_attn_bu)
    small[:, BV0:BG20] = cols(L0_attn_bv)
    small[:, BG20:CB0] = cols(L0_attn_bg2)
    small[:, CB0:BG10] = cols(L0_attn_conv_b)
    small[:, BG10:CW0] = cols(L0_attn_bg1)
    small[:, CW0:CW0 + 3 * DC] = cols(np.asarray(L0_attn_conv_w)[:, 0, :])

    arrays = {
        "x": L0_attn_x,
        "wuT": np.asarray(L0_attn_Wu).T,
        "wvT": np.asarray(L0_attn_Wv).T,
        "wg1T": np.asarray(L0_attn_Wg1).T,
        "wg2T": np.asarray(L0_attn_Wg2).T,
        "small": small,
        "wi": L0_ffn_wi,
        "wo": L0_ffn_wo,
    }
    nc = bacc.Bacc("TRN2", target_bir_lowering=False, num_devices=1)
    sent, args = {}, []
    for name, a in arrays.items():
        a = np.ascontiguousarray(a)
        sent[f"in_{name}"] = a
        args.append(nc.dram_tensor(f"in_{name}", a.shape, mybir.dt.from_np(a.dtype), kind="ExternalInput").ap())
    out = nc.dram_tensor("out_x", (T + SLOTS, D), F32, kind="ExternalOutput").ap()
    build_kernel(nc, *args, out)
    return run_bass_kernel_spmd(nc, [sent], core_ids=[0]).results[0]["out_x"][0:T].reshape(BATCH, SEQ, D)
```
